# Optimizing a Trainium2 kernel written in Bass

```python
import numpy as np
import jax
import jax.numpy as jnp

def _softmax(x, axis=-1):
    return jax.nn.softmax(x, axis=axis)

def _gelu(x):
    return jax.nn.gelu(x, approximate=True)

def _silu(x):
    return jax.nn.silu(x)

def _sigmoid(x):
    return jax.nn.sigmoid(x)

def _layernorm(x, axis=-1, eps=1e-05):
    m = jnp.mean(x, axis=axis, keepdims=True)
    v = jnp.var(x, axis=axis, keepdims=True)
    return (x - m) / jnp.sqrt(v + eps)

def _scatter_add(tgt, idx, src, axis=0):
    return tgt.at[idx].add(src)

def _segment_sum(src, seg, n):
    return jax.ops.segment_sum(src, seg, n)
kernel_name = 'mk_xattn_ffn_d1_seqx_r4_ca4cc9'

def setup_inputs(seed: int=0):
    np.random.seed(seed)
    _w = jnp.asarray

    def _rec_inputs():
        import jax
        import jax.numpy as jnp
        _rk = jax.random.key(seed)
        x = -0.0002928 + 1 * jax.random.normal(jax.random.fold_in(_rk, 1), (2, 512, 256), jnp.float32)
        _lenS = 512 - jax.random.randint(jax.random.fold_in(_rk, 7), (2,), 0, max(1, 512 // 4) + 1, jnp.int32)
        _lenS2 = 1024 - jax.random.randint(jax.random.fold_in(_rk, 8), (2,), 0, max(1, 1024 // 4) + 1, jnp.int32)
        _ctx_1024P = jax.random.normal(jax.random.fold_in(_rk, 11), (2, 16, 256), jnp.float32)
        _ctx_1024c = jax.random.dirichlet(jax.random.fold_in(_rk, 511), 0.3 * jnp.ones((16,), jnp.float32), (2, 1024))
        _ctx_1024t = jnp.einsum('bsk,bkd->bsd', _ctx_1024c, _ctx_1024P)
        _ctx_1024t = _ctx_1024t * jax.lax.rsqrt(jnp.mean(jnp.square(_ctx_1024t)) + 1e-12) * 0.953939
        ctx_1024 = -1.39393e-06 + 0.999914 * (_ctx_1024t + 0.3 * jax.random.normal(jax.random.fold_in(_rk, 611), (2, 1024, 256), jnp.float32))
        return (x, ctx_1024)
    x, ctx_1024 = _rec_inputs()

    def _L0_xattn_setup():
        import jax, jax.numpy as jnp
        import numpy as np
        D_EMB = 256
        N_HEAD = 16
        D_K = D_EMB // N_HEAD

        def _heads(x):
            B, S, _ = x.shape
            return x.reshape(B, S, N_HEAD, D_K).transpose(0, 2, 1, 3)
        key = jax.random.key(seed)
        ks = jax.random.split(key, 11)
        B, S = (2, 512)
        s = 1.0 / np.sqrt(D_EMB)
        inp = {'Q': jax.random.normal(ks[0], (B, S, D_EMB), jnp.float32), 'K': jax.random.normal(ks[1], (B, S, D_EMB), jnp.float32), 'V': jax.random.normal(ks[2], (B, S, D_EMB), jnp.float32), 'W_Q': jax.random.normal(ks[3], (D_EMB, D_EMB), jnp.float32) * s, 'b_Q': jax.random.normal(ks[4], (D_EMB,), jnp.float32) * s, 'W_K': jax.random.normal(ks[5], (D_EMB, D_EMB), jnp.float32) * s, 'b_K': jax.random.normal(ks[6], (D_EMB,), jnp.float32) * s, 'W_V': jax.random.normal(ks[7], (D_EMB, D_EMB), jnp.float32) * s, 'b_V': jax.random.normal(ks[8], (D_EMB,), jnp.float32) * s, 'W_O': jax.random.normal(ks[9], (D_EMB, D_EMB), jnp.float32) * s, 'b_O': jax.random.normal(ks[10], (D_EMB,), jnp.float32) * s}
        return inp
    _L0_xattn_all = _L0_xattn_setup()
    _L0_xattn_in = {k: v for k, v in _L0_xattn_all.items() if k in ('W_Q', 'b_Q', 'W_K', 'b_K', 'W_V', 'b_V', 'W_O', 'b_O')}
    del _L0_xattn_all

    def _L0_ffn_setup():
        import jax, jax.numpy as jnp
        import numpy as np
        D_MODEL = 256
        H_SHARED = 512
        H_ROUTED = 256
        N_EXPERTS = 8
        TOP_K = 2
        key = jax.random.key(seed)
        ks = jax.random.split(key, 8)
        B, T = (2, 512)
        sc_d = 1.0 / np.sqrt(D_MODEL)
        sc_hs = 1.0 / np.sqrt(H_SHARED)
        sc_hr = 1.0 / np.sqrt(H_ROUTED)
        return {'x': jax.random.normal(ks[0], (B, T, D_MODEL), dtype=jnp.float32), 'router_w': jax.random.normal(ks[1], (N_EXPERTS, D_MODEL), dtype=jnp.float32) * sc_d, 'router_bias': jnp.zeros((N_EXPERTS,), dtype=jnp.float32), 'sw1': jax.random.normal(ks[2], (D_MODEL, H_SHARED), dtype=jnp.float32) * sc_d, 'sw3': jax.random.normal(ks[3], (D_MODEL, H_SHARED), dtype=jnp.float32) * sc_d, 'sw2': jax.random.normal(ks[4], (H_SHARED, D_MODEL), dtype=jnp.float32) * sc_hs, 'ew1': jax.random.normal(ks[5], (N_EXPERTS, D_MODEL, H_ROUTED), dtype=jnp.float32) * sc_d, 'ew2': jax.random.normal(ks[6], (N_EXPERTS, H_ROUTED, D_MODEL), dtype=jnp.float32) * sc_hr}
    _L0_ffn_all = _L0_ffn_setup()
    _L0_ffn_in = {k: v for k, v in _L0_ffn_all.items() if k in ('router_w', 'router_bias', 'sw1', 'sw3', 'sw2', 'ew1', 'ew2')}
    del _L0_ffn_all
    return {'x': x, 'ctx_1024': ctx_1024, 'L0_xattn_W_Q': _L0_xattn_in['W_Q'], 'L0_xattn_b_Q': _L0_xattn_in['b_Q'], 'L0_xattn_W_K': _L0_xattn_in['W_K'], 'L0_xattn_b_K': _L0_xattn_in['b_K'], 'L0_xattn_W_V': _L0_xattn_in['W_V'], 'L0_xattn_b_V': _L0_xattn_in['b_V'], 'L0_xattn_W_O': _L0_xattn_in['W_O'], 'L0_xattn_b_O': _L0_xattn_in['b_O'], 'L0_ffn_router_w': _L0_ffn_in['router_w'], 'L0_ffn_router_bias': _L0_ffn_in['router_bias'], 'L0_ffn_sw1': _L0_ffn_in['sw1'], 'L0_ffn_sw3': _L0_ffn_in['sw3'], 'L0_ffn_sw2': _L0_ffn_in['sw2'], 'L0_ffn_ew1': _L0_ffn_in['ew1'], 'L0_ffn_ew2': _L0_ffn_in['ew2']}

def reference(x, ctx_1024, L0_xattn_W_Q, L0_xattn_b_Q, L0_xattn_W_K, L0_xattn_b_K, L0_xattn_W_V, L0_xattn_b_V, L0_xattn_W_O, L0_xattn_b_O, L0_ffn_router_w, L0_ffn_router_bias, L0_ffn_sw1, L0_ffn_sw3, L0_ffn_sw2, L0_ffn_ew1, L0_ffn_ew2):
    import jax
    import jax.numpy as jnp

    def _L0_xattn_ref(Q, K, V, W_Q, b_Q, W_K, b_K, W_V, b_V, W_O, b_O):
        import jax, jax.numpy as jnp
        import numpy as np
        D_EMB = 256
        N_HEAD = 16
        D_K = D_EMB // N_HEAD

        def _heads(x):
            B, S, _ = x.shape
            return x.reshape(B, S, N_HEAD, D_K).transpose(0, 2, 1, 3)
        q = _heads(Q @ W_Q.T + b_Q)
        k = _heads(K @ W_K.T + b_K)
        v = _heads(V @ W_V.T + b_V)
        scale = 1.0 / jnp.sqrt(jnp.asarray(D_K, q.dtype))
        scores = jnp.einsum('bhqd,bhkd->bhqk', q, k) * scale
        probs = jax.nn.softmax(scores, axis=-1)
        attn = jnp.einsum('bhqk,bhkd->bhqd', probs, v)
        B, H, S, d = attn.shape
        attn = attn.transpose(0, 2, 1, 3).reshape(B, S, H * d)
        return attn @ W_O.T + b_O

    def _L0_ffn_ref(x, router_w, router_bias, sw1, sw3, sw2, ew1, ew2):
        import jax, jax.numpy as jnp
        import numpy as np
        D_MODEL = 256
        H_SHARED = 512
        H_ROUTED = 256
        N_EXPERTS = 8
        TOP_K = 2
        B, T, C = x.shape
        xf = x.reshape(-1, C)
        shared_out = jax.nn.silu(xf @ sw1) * (xf @ sw3) @ sw2
        s = jax.nn.sigmoid((xf @ router_w.T).astype(jnp.float32))
        sel_scores = s + router_bias.astype(jnp.float32)
        _, topk_idx = jax.lax.top_k(sel_scores, TOP_K)
        s_sel = jnp.take_along_axis(s, topk_idx, axis=1)
        denom = s_sel.sum(axis=1, keepdims=True)
        gates = jnp.where(denom > 1e-09, s_sel / (denom + 1e-09), 1.0 / TOP_K).astype(x.dtype)
        one_hot = jax.nn.one_hot(topk_idx, N_EXPERTS, dtype=x.dtype)
        comb = jnp.einsum('nke,nk->ne', one_hot, gates)
        h = jax.nn.gelu(jnp.einsum('nd,edh->neh', xf, ew1), approximate=False)
        y = jnp.einsum('neh,ehd->ned', h, ew2)
        routed_out = jnp.einsum('ned,ne->nd', y, comb)
        return (shared_out + routed_out).reshape(B, T, C)
    x = x + _L0_xattn_ref(_layernorm(x, axis=-1), ctx_1024, ctx_1024, L0_xattn_W_Q, L0_xattn_b_Q, L0_xattn_W_K, L0_xattn_b_K, L0_xattn_W_V, L0_xattn_b_V, L0_xattn_W_O, L0_xattn_b_O)
    x = x + _L0_ffn_ref(_layernorm(x, axis=-1), L0_ffn_router_w, L0_ffn_router_bias, L0_ffn_sw1, L0_ffn_sw3, L0_ffn_sw2, L0_ffn_ew1, L0_ffn_ew2)
    return x

_drawn_inputs = setup_inputs


def setup_inputs(seed=0):
    import zlib

    import numpy as np

    out = dict(_drawn_inputs(seed))
    spreads = {'L0_ffn_router_bias': (0.0, 0.1)}
    factors = {}
    for name, (base, spread) in spreads.items():
        noise = np.random.default_rng([zlib.crc32(name.encode()), seed]).standard_normal(out[name].shape)
        drawn = base * np.exp(spread * noise) if base else spread * noise
        out[name] = jnp.asarray(drawn.astype(out[name].dtype))
    for name, factor in factors.items():
        out[name] = (out[name] * factor).astype(out[name].dtype)
    return out
```

```python
from contextlib import ExitStack

import concourse.bass as bass
from concourse import mybir

F32 = mybir.dt.float32
F32R = mybir.dt.float32r
BF16 = mybir.dt.bfloat16
ALU = mybir.AluOpType
ACT = mybir.ActivationFunctionType
AX = mybir.AxisListType

P = 128
B, S, T, D = 2, 512, 1024, 256
NH, DK = 16, 16
NE, HS = 8, 512
N = 512
KT = D // P
GH = 4
NG = B * NH // GH
HG = NH // GH
QT = S // P
KP = T // P // 2
UG = GH * KP
NU = NG * UG
LEAD = 20
TERMS = 6
QPARTS = (0, 0, 0, 1, 1, 2)
KROWS = TERMS * DK
EPS = 1e-5
SLOTS = 3
PR = 8
HR = 5


def xattn_ffn(nc, x, ctxT, bqkT, wqT, wkT, wvT, bv, woT, bo, rwT, rbias, sw1, sw3, sw2, ew1, ew2, out):
    jobs = []
    for b in range(B):
        jobs += [("T", b, kt, 0) for kt in range(KT)]
        for m in range(2):
            jobs += [("K", b, m, 0), ("K", b, m, 1), ("Q", b, m, 0)]
        jobs += [("V", b, i, 0) for i in range(4)]
    NJ = len(jobs)
    kq_jobs = [j for j in jobs if j[0] in "KQ"]
    kq_of = {j: c for c, j in enumerate(kq_jobs)}

    def around_unit(n):
        todo = []
        m = n + LEAD
        if m < NU:
            todo += [("max", m)]
        g1 = (m - UG - 1) // UG
        if (m - UG - 1) % UG == 0 and g1 < NG:
            todo += [("negmax", g1)]
        if n % 2 == 1 and n >= 5:
            q = n // 4 - 1
            if q < NU // 4:
                todo += [("pv", q, (n % 4) // 2)]
        g, r = n // UG - 1, n % UG
        if 0 <= g < NG:
            if r == 3:
                todo += [("evac", g)]
            if r == 6:
                todo += [("sums", g)]
            if r == 9:
                todo += [("norm", g)]
            if r == 12 and g % HG == HG - 1:
                todo += [("oproj", g // HG)]
        return todo

    before = []
    m = 0
    for n, j in enumerate(jobs):
        before.append(("job", n))
        if n >= 10 and m < LEAD:
            before.append(("max", m))
            m += 1
            if m == UG + 2:
                before.append(("negmax", 0))
    while m < LEAD:
        before.append(("max", m))
        m += 1
        if m == UG + 2:
            before.append(("negmax", 0))
    steps = list(before)
    for n in range(NU + 13):
        if n < NU:
            steps.append(("unit", n))
        steps += around_unit(n)

    ring_at, count = {}, 0
    for st in steps:
        if st[0] in ("max", "negmax", "sums", "oproj"):
            ring_at[st] = count
            count += 2 if st[0] in ("max", "oproj") else 1
    NR = count

    pairs = [(tb, k) for tb in range(2) for k in range(4 + NE)]
    ffn = []
    for p, (tb, k) in enumerate(pairs):
        ffn.append(("h", p))
        if k == 4:
            ffn.append(("y", tb * (NE + 1)))
        elif k > 4:
            ffn.append(("y", tb * (NE + 1) + k - 4))
        elif k == 0 and tb > 0:
            ffn.append(("y", tb * (NE + 1) - 1))
    ffn.append(("y", 2 * (NE + 1) - 1))

    def y_of_entry(i):
        tb, k = i // (4 + 2 * NE), i % (4 + 2 * NE)
        return tb * (NE + 1) + (0 if k < 4 else 1 + (k - 4) // 2)

    def entry_of_pair(p):
        tb, k = pairs[p]
        return tb * (4 + 2 * NE) + (k if k < 4 else 4 + 2 * (k - 4))

    NSW = 6
    NCH = NSW + 2 * 2 * NE
    sw_src = [sw1[0:P, :], sw1[P:D, :], sw3[0:P, :], sw3[P:D, :],
              sw2[0:2 * P, :].rearrange("(k p) n -> p k n", p=P), sw2[2 * P:, :].rearrange("(k p) n -> p k n", p=P)]
    EARLY = NSW + 8

    def chunk_src(c):
        if c < NSW:
            return sw_src[c]
        q = (c - NSW) // 2 % NE
        return (ew1, ew2)[(c - NSW) % 2][q].rearrange("(k p) n -> p k n", p=P)

    with ExitStack() as ctx:
        def sb(name, shape, dt):
            return ctx.enter_context(nc.sbuf_tensor(name, shape, dt))

        def sem(name):
            return ctx.enter_context(nc.semaphore(name))

        psum = ctx.enter_context(nc.psum_tensor("psum", [P, 8, N], F32))
        bank = [psum[:, i, :] for i in range(8)]
        ring = bank[4:7]
        acc = bank[7]

        x_sb = sb("x_sb", [P, 8, D], F32)
        R1 = sb("R1", [P, 8, 1024], F32R)
        SWH = sb("SWH", [P, NSW, 1024], F32R)
        WH = sb("WH", [P, 10, N], F32R)
        XT = sb("XT", [P, 8, N], F32R)
        PB = sb("PB", [P, PR, 2 * N], F32)
        VA = sb("VA", [P, B, 8, NH, DK + 1], F32)
        QS = [sb(f"QS{i}", [P, GH, S], BF16) for i in range(SLOTS)]
        KS = [sb(f"KS{i}", [P, GH, T], BF16) for i in range(SLOTS)]
        RAW = sb("RAW", [P, 2, N], F32)
        TMP = sb("TMP", [P, 4, N], F32)
        PARTS = sb("PARTS", [P, 2, 3, N], BF16)
        bv_sb = sb("bv_sb", [P, D], F32)
        bo_sb = sb("bo_sb", [P, D], F32)
        bqk = sb("bqk", [P, 4], F32)
        rw_raw = sb("rw_raw", [P, KT, NE], F32)
        rw = sb("rw", [P, 2, KT, NE], F32R)
        rb_sb = sb("rb_sb", [P, NE], F32)
        ident = sb("ident", [P, P], F32)
        identb = sb("identb", [P, P], BF16)
        sel = sb("sel", [P, P], F32)
        stats = sb("stats", [P, 8, 6], F32)
        mv = sb("mv", [P, 8, 2], F32)
        ve = sb("ve", [P, 8], F32)
        lnv = sb("lnv", [P, 8], F32)
        rstd0 = sb("rstd0", [P, 8], F32)
        nt1 = sb("nt1", [P, 8], F32)
        nt2 = sb("nt2", [P, 8], F32)
        rstd = sb("rstd", [P, 8], F32)
        mx = sb("mx", [P, 2, GH, QT, 2], F32)
        negm = sb("negm", [P, GH, QT], F32)
        nhl = sb("nhl", [P, 2, QT, 2, GH], BF16)
        one8 = sb("one8", [P, 4 * NE], F32)
        rs = sb("rs", [P, 8, 8], F32)
        desc = sb("desc", [P, NE], F32)

        xn = KS[2][:, :, :].bitcast(F32).rearrange("p a b -> p (a b)").rearrange("p (t d) -> p t d", d=D)
        craw = PB[:, 0:4, :].rearrange("p a b -> p (a b)").rearrange("p (k t) -> p k t", k=KT)
        wraw = PB[:, 4:6, :].rearrange("p a b -> p (a b)").rearrange("p (w k n) -> p w k n", w=4, k=KT)
        woraw = PB[:, 6, :].rearrange("p (g n) -> p g n", g=HG)
        R1f = R1[:, :, :].rearrange("p a b -> p (a b)")
        ctx_hl = [R1f[:, i * 4096:(i + 1) * 4096].rearrange("p (k t) -> p k t", k=KT) for i in range(2)]
        w_hl = [[WH[:, 2 * w + i, :].rearrange("p (k n) -> p k n", k=KT) for i in range(2)] for w in range(3)]
        WK, WQ, WV = 0, 1, 2
        wo_hl = [WH[:, 6 + 2 * i:8 + 2 * i, :].rearrange("p a b -> p (a b)").rearrange("p (g n) -> p g n", g=HG)
                 for i in range(2)]
        xt_hl = [XT[:, 4 * i:4 * i + 4, :].rearrange("p (k b) n -> p k b n", b=2) for i in range(2)]
        U, RC = TMP[:, 0, :], TMP[:, 1, :]
        nrow = TMP[0:2 * GH, 2, :].bitcast(BF16).rearrange("p (b n) -> p b n", b=2)
        rt = PB[:, 0, 0:12 * 8 * NE].rearrange("p (i t e) -> p i t e", i=12, e=NE)

        qs_d = nc.dram_tensor("qs_d", (B, HG, GH, TERMS, DK, S), BF16, kind="Internal").ap()
        ks_d = nc.dram_tensor("ks_d", (B, HG, GH, 3, DK, T), BF16, kind="Internal").ap()

        ld_x = sem("ld_x")
        ld_ctx = [sem(f"ld_ctx{b}") for b in range(B)]
        ld_w = [sem(f"ld_w{w}") for w in range(3)]
        ld_wo = sem("ld_wo")
        ld_bias = sem("ld_bias")
        ld_rw = sem("ld_rw")
        consts = sem("consts")
        const_step = sem("const_step")
        ones2 = sem("ones2")
        acc_zero = sem("acc_zero")
        var_ready = sem("var_ready")
        rstd_guess = sem("rstd_guess")
        act_chain = sem("act_chain")
        dve_chain = sem("dve_chain")
        xn_ready = sem("xn_ready")
        split_hi = sem("split_hi")
        split_lo = sem("split_lo")
        pool_split = sem("pool_split")
        pool_chain = sem("pool_chain")
        jobs_done = sem("jobs_done")
        job_free = [sem(f"job_free{i}") for i in range(4)]
        xt_hi = sem("xt_hi")
        v_ready = sem("v_ready")
        kq_hi = sem("kq_hi")
        kq_mid = sem("kq_mid")
        kq_split = sem("kq_split")
        kq_stored = [sem(f"kq_stored{c}") for c in range(len(kq_jobs))]
        stk_loaded = [sem(f"stk_loaded{i}") for i in range(SLOTS)]
        bias_loaded = [sem(f"bias_loaded{i}") for i in range(2)]
        ring_full = sem("ring_full")
        ring_empty = sem("ring_empty")
        negm_ready = sem("negm_ready")
        scores_done = sem("scores_done")
        exp_done = sem("exp_done")
        pv_done = sem("pv_done")
        u_ready = sem("u_ready")
        an_ready = sem("an_ready")
        a_hi = sem("a_hi")
        a_lo = sem("a_lo")
        bo_added = sem("bo_added")
        wraw_loaded = [sem(f"wraw_loaded{i}") for i in range(2)]
        w_split = sem("w_split")
        t2_done = sem("t2_done")
        t2_hi = sem("t2_hi")
        t2_lo = sem("t2_lo")
        rt_full = sem("rt_full")
        rt_exp = sem("rt_exp")
        h_full = sem("h_full")
        h_free = [sem(f"h_free{i}") for i in range(2)]
        g_ready = sem("g_ready")
        ht_ready = sem("ht_ready")
        y_full = sem("y_full")
        y_free = sem("y_free")
        stored = sem("stored")

        block = ctx.enter_context(nc.Block())

        def kq_count(b, m):
            return 3 * (2 * b + m)

        @block.sync
        def _(sp):
            sp.dma_start(x_sb[:, :, :], x.rearrange("(t p) d -> p t d", p=P)).then_inc(ld_x, 16)
            cT = ctxT.rearrange("(k p) t -> p k t", p=P)
            sp.dma_start(wraw[:, WK], wkT.rearrange("(k p) n -> p k n", p=P)).then_inc(ld_w[WK], 16)
            sp.dma_start(craw[:, :, 0:T], cT[:, :, 0:T]).then_inc(ld_ctx[0], 16)
            sp.dma_start(wraw[:, WQ], wqT.rearrange("(k p) n -> p k n", p=P)).then_inc(ld_w[WQ], 16)
            sp.dma_start(wraw[:, WV], wvT.rearrange("(k p) n -> p k n", p=P)).then_inc(ld_w[WV], 16)
            sp.dma_start(craw[:, :, T:], cT[:, :, T:]).then_inc(ld_ctx[1], 16)

            def load_stack(g):
                b, hg, s = g // HG, g % HG, g % SLOTS
                if hg % 2 == 0:
                    for c in range(kq_count(b, hg // 2), kq_count(b, hg // 2) + 3):
                        sp.wait_ge(kq_stored[c], 16 * (3 if c % 3 < 2 else TERMS))
                if g == 2:
                    sp.wait_ge(jobs_done, jobs.index(("T", 1, 1, 0)) + 1)
                if g >= SLOTS:
                    sp.wait_ge(scores_done, UG * (g - SLOTS + 1))
                sp.dma_start(QS[s][0:KROWS, :, :], qs_d[b, hg].rearrange("j p d t -> (p d) j t"))\
                    .then_inc(stk_loaded[s], 16)
                row = 0
                for n in (3, 2, 1):
                    sp.dma_start(KS[s][row:row + n * DK, :, :],
                                 ks_d[b, hg][:, 0:n].rearrange("j p d t -> (p d) j t")).then_inc(stk_loaded[s], 16)
                    row += n * DK

            def load_bias(g):
                sp.wait_ge(ring_empty, ring_at[("negmax", g)] + 1)
                for c in range(2):
                    sp.dma_start(QS[g % SLOTS][KROWS + c:KROWS + c + 1, :, :],
                                 nrow[GH * c:GH * c + GH, g % 2, :]).then_inc(bias_loaded[g % 2], 16)

            def load_chunk(c):
                if c >= 2:
                    sp.wait_ge(w_split, c - 1)
                dst = RAW[:, c % 2, :]
                if c >= 4:
                    dst = dst.rearrange("p (k n) -> p k n", k=2)
                sp.dma_start(dst, chunk_src(c)).then_inc(wraw_loaded[c % 2], 16)

            for c, (kind, b, m, tb) in enumerate(kq_jobs):
                sp.wait_ge(kq_split, c + 1)
                for t in range(TERMS if kind == "Q" else 3):
                    part = QPARTS[t] if kind == "Q" else t
                    if kind == "Q":
                        dst = qs_d[b, 2 * m:2 * m + 2, :, t]
                    else:
                        dst = ks_d[b, 2 * m:2 * m + 2, :, t, :, tb * N:(tb + 1) * N]
                    sp.dma_start(dst.rearrange("l j d t -> (l j) d t"), PARTS[:, c % 2, part, :])\
                        .then_inc(kq_stored[c], 16)
                if c == 2:
                    load_stack(0)
                    load_stack(1)
                if c == 5:
                    load_stack(2)
            load_bias(0)
            for c in range(EARLY):
                load_chunk(c)
            for g in range(NG):
                if g + 1 < NG:
                    load_bias(g + 1)
                if g + SLOTS < NG:
                    load_stack(g + SLOTS)
            for c in range(EARLY, NCH):
                load_chunk(c)
            for tb in range(2):
                sp.wait_ge(y_free, (tb + 1) * (NE + 1))
                sp.dma_start(out.rearrange("(t p) d -> p t d", p=P)[:, 4 * tb:4 * tb + 4, :],
                             x_sb[:, 4 * tb:4 * tb + 4, :]).then_inc(stored, 16)
            sp.wait_ge(stored, 32)

        @block.gpsimd
        def _(pool):
            k = 0
            for t in (ident, identb, sel):
                pool.memset(t[:, :], 0.0).then_inc(const_step, 1)
            pool.memset(woraw, 0.0).then_inc(const_step, 1)
            pool.memset(VA[:, :, :, :, DK:DK + 1], 1.0).then_inc(consts, 1)
            for e in range(NE):
                pool.memset(desc[:, e:e + 1], float(NE - e)).then_inc(consts, 1)
            pool.wait_ge(const_step, 3)
            for t in (ident, identb):
                pool.affine_select(out=t[:, :], in_=t[:, :], compare_op=ALU.not_equal, fill=1.0, base=0,
                                   pattern=[[-1, P]], channel_multiplier=1).then_inc(consts, 1)
            sv = sel[:, :].rearrange("p (a i) -> p a i", a=4)
            pool.affine_select(out=sv, in_=sv, compare_op=ALU.not_equal, fill=1.0, base=-DK,
                               pattern=[[-32, 4], [0, 32]], channel_multiplier=1).then_inc(consts, 1)

            pool.wait_ge(consts, 1 + NE + 3)
            for s in range(2):
                pool.memset(KS[s][KROWS:KROWS + 2, :, :], 1.0).then_inc(consts, 1)
                pool.wait_ge(consts, 1 + NE + 3 + s + 1)

            pool.wait_ge(ld_rw, 32)
            pool.tensor_scalar(rw[:, 0], rw_raw[:, :, :], 1.0, 1.0, ALU.mult, ALU.mult).then_inc(pool_chain, 1)
            pool.wait_ge(ld_wo, 16 * GH)
            pool.tensor_scalar(wo_hl[0], woraw, 1.0, 1.0, ALU.mult, ALU.mult).then_inc(pool_chain, 1)
            pool.wait_ge(pool_chain, 2)
            pool.tensor_tensor(rw[:, 1], rw_raw[:, :, :], raw(rw[:, 0]), ALU.subtract).then_inc(pool_split, 1)
            pool.tensor_tensor(wo_hl[1], woraw, raw(wo_hl[0]), ALU.subtract).then_inc(pool_split, 1)

            for c in range(len(kq_jobs)):
                pool.wait_ge(kq_mid, c + 1)
                pool.tensor_tensor(PARTS[:, c % 2, 2, :], TMP[:, c % 2, :], PARTS[:, c % 2, 1, :], ALU.subtract)\
                    .then_inc(kq_split, 1)
            pool.wait_ge(jobs_done, jobs.index(("T", 1, 1, 0)) + 1)
            pool.wait_ge(kq_split, len(kq_jobs))
            pool.memset(KS[2][KROWS:KROWS + 2, :, :], 1.0).then_inc(ones2, 1)
            pool.wait_ge(ones2, 1)
            pool.wait_ge(xn_ready, 8)
            pool.wait_ge(ld_bias, 48)
            for t in range(8):
                pool.tensor_tensor(x_sb[:, t, :], x_sb[:, t, :], bo_sb[:, :], ALU.add).then_inc(bo_added, 1)

            def split_chunk(c):
                pool.wait_ge(wraw_loaded[c % 2], 16 * (c // 2 + 1))
                if c < NSW:
                    hi, lo = SWH[:, c, 0:N], SWH[:, c, N:]
                else:
                    s = (c - NSW) % 8
                    hi, lo = R1[:, s, 0:N], R1[:, s, N:]
                    if c == NSW:
                        pool.wait_ge(jobs_done, NJ)
                    if c >= EARLY:
                        q = (c - EARLY) // 2
                        pool.wait_ge(y_full, (q // NE) * (NE + 1) + 2 + q % NE)
                pool.tensor_scalar(hi, RAW[:, c % 2, :], 1.0, 1.0, ALU.mult, ALU.mult).then_inc(pool_chain, 1)
                pool.wait_ge(pool_chain, 3 + c)
                pool.tensor_tensor(lo, RAW[:, c % 2, :], raw(hi), ALU.subtract).then_inc(w_split, 1)

            for c in range(EARLY):
                split_chunk(c)
            for g in range(NG):
                pool.wait_ge(ring_empty, ring_at[("sums", g)] + 1)
                pool.wait_ge(u_ready, g + 1)
                pool.tensor_tensor(RC, RC, U, ALU.mult).then_inc(an_ready, 1)
                pool.wait_ge(a_hi, g + 1)
                pool.tensor_tensor(XT[:, 2 * (g % HG) + 1, :], RC, raw(XT[:, 2 * (g % HG), :]), ALU.subtract)\
                    .then_inc(a_lo, 1)
            for c in range(EARLY, NCH):
                split_chunk(c)

        @block.scalar
        def _(act):
            chain = [0]

            def link(ins):
                chain[0] += 1
                ins.then_inc(act_chain, 1)
                act.wait_ge(act_chain, chain[0])

            act.dma_start(bqk[:, :], bqkT).then_inc(ld_bias, 16)
            act.dma_start(bv_sb[:, :], bv.rearrange("(a n) -> a n", a=1).broadcast_to([P, D])).then_inc(ld_bias, 16)
            act.dma_start(bo_sb[:, :], bo.rearrange("(a n) -> a n", a=1).broadcast_to([P, D])).then_inc(ld_bias, 16)
            act.dma_start(rw_raw[:, :, :], rwT.rearrange("(k p) n -> p k n", p=P)).then_inc(ld_rw, 16)
            act.dma_start(rb_sb[:, :], rbias.rearrange("(a n) -> a n", a=1).broadcast_to([P, NE])).then_inc(ld_rw, 16)
            act.wait_ge(const_step, 4)
            for j in range(GH):
                act.dma_start(woraw[32 * j:32 * j + DK, :, :],
                              woT.rearrange("(g j d) n -> j d g n", g=HG, j=GH)[j]).then_inc(ld_wo, 16)

            def first_rstd(n):
                act.wait_ge(var_ready, n)
                link(act.activation(lnv[:, :], ve[:, :], ACT.Ln))
                act.activation(rstd0[:, :], lnv[:, :], ACT.Exp, scale=-0.5).then_inc(rstd_guess, 1)

            first_rstd(1)
            hi_items = [("w", WK), ("c", 0, 0), ("c", 0, 1), ("w", WQ), ("w", WV), ("c", 1, 0), ("c", 1, 1)]
            for i, it in enumerate(hi_items):
                if it[0] == "w":
                    act.wait_ge(ld_w[it[1]], 16)
                    act.activation(w_hl[it[1]][0], wraw[:, it[1]], ACT.Copy).then_inc(split_hi, 1)
                else:
                    act.wait_ge(ld_ctx[it[1]], 16)
                    c0 = it[1] * T + it[2] * N
                    act.activation(ctx_hl[0][:, :, c0:c0 + N], craw[:, :, c0:c0 + N], ACT.Copy).then_inc(split_hi, 1)
            act.wait_ge(ld_bias, 48)

            def job(n):
                kind, b, m, tb = jobs[n]
                if kind == "T":
                    act.wait_ge(jobs_done, n + 1)
                    act.activation(xt_hl[0][:, m, b, :], bank[n % 4][:, :], ACT.Copy).then_inc(xt_hi, 1)
                if kind in "KQ":
                    c = kq_of[jobs[n]]
                    act.wait_ge(jobs_done, n + 1)
                    if c >= 2:
                        act.wait_ge(kq_split, c - 1)
                        act.wait_ge(kq_stored[c - 2], 16 * (TERMS if (c - 2) % 3 == 2 else 3))
                    bias = bqk[:, m:m + 1] if kind == "Q" else bqk[:, 2 + m:3 + m]
                    act.activation(TMP[:, c % 2, :], bank[n % 4][:, :], ACT.Identity, bias=bias).then_inc(kq_hi, 1)
                    act.activation(PARTS[:, c % 2, 0, :], bank[n % 4][:, :], ACT.Identity, bias=bias)\
                        .then_inc(job_free[n % 4], 1)

            def unit(n):
                act.wait_ge(scores_done, n + 1)
                if n >= PR:
                    act.wait_ge(pv_done, 2 * (n // 4) - 2)
                elif n == 0:
                    act.wait_ge(pool_split, 2)
                    act.wait_ge(split_lo, len(hi_items))
                e = 2 * (n % 2)
                act.activation(PB[:, n % PR, :], psum[:, e:e + 2, :].rearrange("p a b -> p (a b)"), ACT.Exp,
                               scale=DK ** -0.5).then_inc(exp_done, 1)

            for st in steps:
                if st[0] == "job":
                    job(st[1])
                elif st[0] == "unit":
                    unit(st[1])
                elif st[0] == "evac":
                    g = st[1]
                    act.wait_ge(pv_done, 2 * (g + 1) * KP)
                    if g:
                        act.wait_ge(an_ready, g)
                    else:
                        act.wait_ge(kq_split, len(kq_jobs))
                        act.wait_ge(acc_zero, 1)
                    act.activation(U, acc[:, :], ACT.Copy).then_inc(u_ready, 1)
                elif st[0] == "norm":
                    g = st[1]
                    act.wait_ge(an_ready, g + 1)
                    if g == 0:
                        act.wait_ge(jobs_done, NJ)
                    if g == HG:
                        act.wait_ge(ring_full, ring_at[("oproj", 0)] + 2)
                    act.activation(XT[:, 2 * (g % HG), :], RC, ACT.Copy).then_inc(a_hi, 1)

            first_rstd(2)
            for i in range(4):
                act.wait_ge(t2_done, i + 1)
                act.activation(xt_hl[0][:, i % 2, i // 2, :], bank[i][:, :], ACT.Copy).then_inc(t2_hi, 1)
            act.wait_ge(rt_full, 1)
            act.activation(rt[:, 0], bank[4][:, 0:8 * NE].rearrange("p (t e) -> p t e", e=NE), ACT.Exp, scale=-1.0)\
               .then_inc(rt_exp, 1)
            for p, (tb, k) in enumerate(pairs):
                act.wait_ge(h_full, p + 1)
                b0 = 2 * (p % 2)
                e0 = entry_of_pair(p)
                for i in range(1 if k < 4 else 2):
                    e = e0 + i
                    if e >= 4:
                        act.wait_ge(ht_ready, e - 3)
                    func = ACT.Silu if k < 4 else ACT.Gelu
                    g = act.activation(TMP[:, e % 4, :], bank[b0 + i][:, :], func)
                    g.then_inc(g_ready, 1)

        @block.vector
        def _(dve):
            chain = [0]

            def link(ins):
                chain[0] += 1
                ins.then_inc(dve_chain, 1)
                dve.wait_ge(dve_chain, chain[0])

            dve.memset(acc[:, :], 0.0).then_inc(acc_zero, 1)

            def layer_stats(n):
                for t in range(8):
                    last = dve.bn_stats(stats[:, t, :], x_sb[:, t, :])
                link(last)
                for t in range(8):
                    last = dve.bn_aggr(mv[:, t, :], stats[:, t, :])
                link(last)
                dve.tensor_scalar(ve[:, :], mv[:, :, 1], EPS, None, ALU.add).then_inc(var_ready, 1)
                dve.wait_ge(rstd_guess, n)
                link(dve.tensor_tensor(nt1[:, :], rstd0[:, :], rstd0[:, :], ALU.mult))
                link(dve.tensor_tensor(nt2[:, :], nt1[:, :], ve[:, :], ALU.mult))
                link(dve.tensor_scalar(nt1[:, :], nt2[:, :], -0.5, 1.5, ALU.mult, ALU.add))
                link(dve.tensor_tensor(rstd[:, :], rstd0[:, :], nt1[:, :], ALU.mult))

            def normalise(t):
                dve.tensor_scalar(xn[:, t, :], x_sb[:, t, :], mv[:, t, 0:1], rstd[:, t:t + 1],
                                  ALU.subtract, ALU.mult).then_inc(xn_ready, 1)

            dve.wait_ge(ld_x, 16)
            layer_stats(1)
            for t in range(8):
                normalise(t)

            lo_items = [("w", WK), ("c", 0, 0), ("c", 0, 1), ("w", WQ), ("w", WV), ("c", 1, 0), ("c", 1, 1)]

            def split_low(i):
                it = lo_items[i]
                dve.wait_ge(split_hi, i + 1)
                if it[0] == "w":
                    dve.tensor_tensor(w_hl[it[1]][1], wraw[:, it[1]], raw(w_hl[it[1]][0]), ALU.subtract)\
                        .then_inc(split_lo, 1)
                else:
                    c0 = it[1] * T + it[2] * N
                    dve.tensor_tensor(ctx_hl[1][:, :, c0:c0 + N], craw[:, :, c0:c0 + N],
                                      raw(ctx_hl[0][:, :, c0:c0 + N]), ALU.subtract).then_inc(split_lo, 1)

            def job(n):
                kind, b, m, tb = jobs[n]
                if kind == "T":
                    i = 2 * b + m
                    dve.wait_ge(xt_hi, i + 1)
                    dve.tensor_tensor(xt_hl[1][:, m, b, :], bank[n % 4][:, :], raw(xt_hl[0][:, m, b, :]), ALU.subtract)\
                        .then_inc(job_free[n % 4], 1)
                if kind in "KQ":
                    c = kq_of[jobs[n]]
                    dve.wait_ge(kq_hi, c + 1)
                    dve.wait_ge(job_free[n % 4], n // 4 + 1)
                    link(dve.tensor_tensor(TMP[:, c % 2, :], TMP[:, c % 2, :], PARTS[:, c % 2, 0, :], ALU.subtract))
                    dve.tensor_copy(PARTS[:, c % 2, 1, :], TMP[:, c % 2, :]).then_inc(kq_mid, 1)
                if kind == "V":
                    dve.wait_ge(jobs_done, n + 1)
                    if b == 0 and m == 0:
                        dve.wait_ge(ld_bias, 48)
                    src = bank[n % 4][:, :].rearrange("p (t h d) -> p t h d", t=2, h=NH)
                    for t in range(2):
                        last = dve.tensor_tensor(VA[:, b, 2 * m + t, :, 0:DK], src[:, t],
                                                 bv_sb[:, :].rearrange("p (h d) -> p h d", h=NH), ALU.add)
                    last.then_inc(job_free[n % 4], 1)

            def ring_wait(st, i=0):
                dve.wait_ge(ring_full, ring_at[st] + i + 1)
                return ring[(ring_at[st] + i) % 3]

            def maxima(m):
                g, r = m // UG, m % UG
                for half in range(2):
                    src = ring_wait(("max", m), half)
                    dve.tensor_reduce(mx[:, g % 2, r // QT, r % QT, half:half + 1], src[:, :], AX.X, ALU.max)\
                        .then_inc(ring_empty, 1)
                if r == UG - 1:
                    dve.wait_ge(ring_empty, ring_at[("max", m)] + 2)
                    link(dve.tensor_reduce(negm[:, :, :], mx[:, g % 2], AX.X, ALU.max, negate=True))
                    nv = negm[:, :, :].rearrange("p j q -> p q j")
                    link(dve.tensor_copy(nhl[:, g % 2, :, 0, :], nv))
                    dve.tensor_tensor(nhl[:, g % 2, :, 1, :], nv, nhl[:, g % 2, :, 0, :], ALU.subtract)\
                       .then_inc(negm_ready, 1)

            lows_after = {0: 0, 1: 3}
            for st in steps:
                if st[0] == "job":
                    n = st[1]
                    if n == 0:
                        for i in range(3):
                            split_low(i)
                    job(n)
                    if n == 1:
                        split_low(3)
                        split_low(4)
                    if n == 7:
                        split_low(5)
                        split_low(6)
                elif st[0] == "max":
                    maxima(st[1])
                elif st[0] == "negmax":
                    g = st[1]
                    src = ring_wait(st)
                    if g >= 2:
                        dve.wait_ge(bias_loaded[g % 2], 32 * (g // 2))
                    dve.tensor_copy(nrow[:, g % 2, :], src[0:2 * GH, :]).then_inc(ring_empty, 1)
                elif st[0] == "sums":
                    g = st[1]
                    src = ring_wait(st)
                    if g:
                        dve.wait_ge(a_lo, g)
                    dve.reciprocal(RC, src[:, :]).then_inc(ring_empty, 1)
                elif st[0] == "oproj":
                    b = st[1]
                    dve.wait_ge(bo_added, 8)
                    for i in range(2):
                        src = ring_wait(st, i)
                        t = 4 * b + 2 * i
                        dst = x_sb[:, t:t + 2, :]
                        dve.tensor_tensor(dst, src[:, :].rearrange("p (t n) -> p t n", t=2), dst, ALU.add)\
                           .then_inc(ring_empty, 1)

            dve.wait_ge(ring_empty, NR)
            layer_stats(2)
            for t in range(8):
                normalise(t)
            for i in range(4):
                dve.wait_ge(t2_hi, i + 1)
                dve.tensor_tensor(xt_hl[1][:, i % 2, i // 2, :], bank[i][:, :], raw(xt_hl[0][:, i % 2, i // 2, :]),
                                  ALU.subtract).then_inc(t2_lo, 1)
            dve.wait_ge(rt_exp, 1)
            dve.wait_ge(ld_rw, 32)
            dve.wait_ge(consts, 1 + 2 + NE + 3)
            e_, s_, sel_, eq, w_, oh, sl2, w2, oh2, both, prod, comb = (rt[:, i] for i in range(12))
            bc = lambda v: v.broadcast_to([P, 8, NE])
            col = lambda i: rs[:, i, :].rearrange("p (t o) -> p t o", o=1)
            link(dve.tensor_scalar(both, e_, 1.0, None, ALU.add))
            link(dve.reciprocal(s_, both))
            rbv = rb_sb[:, :].rearrange("p (o e) -> p o e", o=1)
            dsv = desc[:, :].rearrange("p (o e) -> p o e", o=1)
            link(dve.tensor_tensor(sel_, s_, bc(rbv), ALU.add))

            def first_max(src, eq, w, oh, i):
                link(dve.tensor_reduce(col(i), src, AX.X, ALU.max))
                link(dve.tensor_tensor(eq, src, bc(col(i)), ALU.is_equal))
                link(dve.tensor_tensor(w, eq, bc(dsv), ALU.mult))
                link(dve.tensor_reduce(col(i + 1), w, AX.X, ALU.max))
                link(dve.tensor_tensor(oh, w, bc(col(i + 1)), ALU.is_equal))

            first_max(sel_, eq, w_, oh, 0)
            link(dve.scalar_tensor_tensor(out=sl2, in0=oh, scalar=-1e30, in1=sel_, op0=ALU.mult, op1=ALU.add))
            first_max(sl2, eq, w2, oh2, 2)
            link(dve.tensor_tensor(both, oh, oh2, ALU.add))
            link(dve.tensor_tensor(prod, both, s_, ALU.mult))
            link(dve.tensor_reduce(col(4), prod, AX.X, ALU.add))
            link(dve.tensor_scalar(col(5), col(4), 1e-9, None, ALU.is_gt))
            link(dve.tensor_scalar(col(6), col(4), 1e-9, None, ALU.add))
            link(dve.reciprocal(col(7), col(6)))
            link(dve.tensor_tensor(col(6), col(7), col(5), ALU.mult))
            link(dve.tensor_scalar(col(7), col(5), -0.5, 0.5, ALU.mult, ALU.add))
            link(dve.tensor_tensor(prod, prod, bc(col(6)), ALU.mult))
            link(dve.tensor_tensor(both, both, bc(col(7)), ALU.mult))
            link(dve.tensor_tensor(comb, prod, both, ALU.add))

            for st in ffn:
                if st[0] == "h":
                    p = st[1]
                    tb, k = pairs[p]
                    for i in range(1 if k < 4 else 2):
                        e = entry_of_pair(p) + i
                        gt = TMP[:, e % 4, :]
                        hi, lo = WH[:, 2 * (e % HR), :], WH[:, 2 * (e % HR) + 1, :]
                        dve.wait_ge(g_ready, e + 1)
                        if k < 4:
                            dve.tensor_tensor(gt, gt, bank[2 * (p % 2) + 1][:, :], ALU.mult).then_inc(h_free[p % 2], 1)
                            dve.wait_ge(h_free[p % 2], shared_before(pairs, p))
                        if e >= HR:
                            dve.wait_ge(y_full, y_of_entry(e - HR) + 1)
                        link(dve.tensor_copy(hi, gt))
                        dve.tensor_tensor(lo, gt, raw(hi), ALU.subtract).then_inc(ht_ready, 1)
                else:
                    y = st[1]
                    tb, k = y // (NE + 1), y % (NE + 1)
                    dve.wait_ge(y_full, y + 1)
                    for t in range(4):
                        src = bank[4 + 2 * (y % 2) + t // 2][:, (t % 2) * D:(t % 2 + 1) * D]
                        dst = x_sb[:, 4 * tb + t, :]
                        if k == 0:
                            last = dve.tensor_tensor(dst, src, dst, ALU.add)
                        else:
                            last = dve.scalar_tensor_tensor(out=dst, in0=src, scalar=comb[:, 4 * tb + t, k - 1:k],
                                                            in1=dst, op0=ALU.mult, op1=ALU.add)
                    last.then_inc(y_free, 1)
                    dve.wait_ge(y_free, y + 1)

        @block.tensor
        def _(pe):
            def product(dst, a_hl, b_hl, first=True, last=True):
                for i, (u, v) in enumerate(((0, 0), (0, 1), (1, 0))):
                    r = pe.matmul(dst, a_hl[u], b_hl[v], start=first and i == 0, stop=last and i == 2)
                return r

            def job(n):
                kind, b, m, tb = jobs[n]
                o = bank[n % 4]
                if n >= 4:
                    pe.wait_ge(job_free[n % 4], n // 4)
                if kind == "T":
                    pe.wait_ge(xn_ready, 4 * b + 4)
                    pe.wait_ge(consts, 1 + 2 + NE + 3)
                    for t in range(4):
                        r = pe.transpose(o[:, t * P:(t + 1) * P], xn[:, 4 * b + t, m * P:(m + 1) * P], ident[:, :])
                elif kind == "K":
                    pe.wait_ge(split_lo, (2 + tb) if b == 0 else 6 + tb)
                    c0 = b * T + tb * N
                    for kt in range(KT):
                        r = product(o[:, :], [w[:, kt, m * P:(m + 1) * P] for w in w_hl[WK]],
                                    [c[:, kt, c0:c0 + N] for c in ctx_hl], kt == 0, kt == KT - 1)
                elif kind == "Q":
                    pe.wait_ge(split_lo, 4)
                    for kt in range(KT):
                        t = jobs.index(("T", b, kt, 0))
                        pe.wait_ge(job_free[t % 4], t // 4 + 1)
                    for kt in range(KT):
                        r = product(o[:, :], [w[:, kt, m * P:(m + 1) * P] for w in w_hl[WQ]],
                                    [t[:, kt, b, :] for t in xt_hl], kt == 0, kt == KT - 1)
                else:
                    pe.wait_ge(split_lo, 5 if b == 0 else 7)
                    for t in range(2):
                        c0 = b * T + (2 * m + t) * P
                        for kt in range(KT):
                            r = product(o[:, t * D:(t + 1) * D], [c[:, kt, c0:c0 + P] for c in ctx_hl],
                                        [w[:, kt, :] for w in w_hl[WV]], kt == 0, kt == KT - 1)
                r.then_inc(jobs_done, 1)

            def ring_wait(st, i=0):
                at = ring_at[st] + i
                if at >= 3:
                    pe.wait_ge(ring_empty, at - 2)
                return ring[at % 3]

            for st in steps:
                if st[0] == "job":
                    job(st[1])
                elif st[0] == "unit":
                    n = st[1]
                    g, r = n // UG, n % UG
                    kp, j = r // GH, r % GH
                    s = g % SLOTS
                    if r == 0:
                        pe.wait_ge(bias_loaded[g % 2], 32 * (g // 2 + 1))
                        if g == 2:
                            pe.wait_ge(ones2, 1)
                        pe.wait_ge(stk_loaded[s], 64 * (g // SLOTS + 1))
                    if n < 2:
                        for i in range(2):
                            pe.wait_ge(job_free[2 * n + i], NJ // 4)
                    else:
                        pe.wait_ge(exp_done, n - 1)
                    for i in range(2):
                        k0 = (2 * kp + i) * P
                        last = pe.matmul(bank[2 * (n % 2) + i][:, :], KS[s][0:KROWS + 2, j, k0:k0 + P],
                                         QS[s][0:KROWS + 2, j, :], start=True, stop=True)
                    last.then_inc(scores_done, 1)
                elif st[0] == "max":
                    m = st[1]
                    g, r = m // UG, m % UG
                    s, j, qt = g % SLOTS, r // QT, r % QT
                    if r == 0:
                        pe.wait_ge(stk_loaded[s], 64 * (g // SLOTS + 1))
                    for half in range(2):
                        o = ring_wait(st, half)
                        pe.matmul(o[:, :], QS[s][0:KROWS, j, qt * P:(qt + 1) * P],
                                  KS[s][0:KROWS, j, half * N:(half + 1) * N], start=True, stop=True)\
                          .then_inc(ring_full, 1)
                elif st[0] == "negmax":
                    g = st[1]
                    o = ring_wait(st)
                    pe.wait_ge(negm_ready, g + 1)
                    for qt in range(QT):
                        last = pe.matmul(o[0:2 * GH, qt * P:(qt + 1) * P],
                                         nhl[:, g % 2, qt].rearrange("p c j -> p (c j)"), identb[:, :],
                                         start=True, stop=True)
                    last.then_inc(ring_full, 1)
                elif st[0] == "pv":
                    q, kk = st[1:]
                    g, kp = q // KP, q % KP
                    if kk == 0:
                        pe.wait_ge(exp_done, 4 * q + 4)
                        if kp == 0:
                            if g:
                                pe.wait_ge(u_ready, g)
                            else:
                                pe.wait_ge(acc_zero, 1)
                    b, hg = g // HG, g % HG
                    for j in range(GH):
                        last = pe.matmul(acc[32 * j:32 * j + DK + 1, :], VA[:, b, 2 * kp + kk, GH * hg + j, :],
                                         PB[:, (4 * q + j) % PR, kk * N:(kk + 1) * N],
                                         start=(kp == 0 and kk == 0), stop=(kp == KP - 1 and kk == 1))
                    last.then_inc(pv_done, 1)
                elif st[0] == "sums":
                    g = st[1]
                    o = ring_wait(st)
                    pe.wait_ge(u_ready, g + 1)
                    pe.matmul(o[:, :], sel[:, :], U, start=True, stop=True).then_inc(ring_full, 1)
                elif st[0] == "oproj":
                    b = st[1]
                    pe.wait_ge(a_lo, HG * (b + 1))
                    pe.wait_ge(pool_split, 2)
                    for i in range(2):
                        o = ring_wait(st, i)
                        for t in range(2):
                            t0 = (2 * i + t) * P
                            for hg in range(HG):
                                last = product(o[:, t * D:(t + 1) * D],
                                               [XT[:, 2 * hg + u, t0:t0 + P] for u in range(2)],
                                               [w[:, hg, :] for w in wo_hl], hg == 0, hg == HG - 1)
                        last.then_inc(ring_full, 1)

            pe.wait_ge(exp_done, NU)
            for i in range(4):
                b, m = i // 2, i % 2
                pe.wait_ge(xn_ready, 8 + 4 * b + 4)
                for t in range(4):
                    r = pe.transpose(bank[i][:, t * P:(t + 1) * P], xn[:, 4 * b + t, m * P:(m + 1) * P], ident[:, :])
                r.then_inc(t2_done, 1)
            pe.wait_ge(t2_lo, 4)
            for t in range(8):
                for kt in range(KT):
                    r = product(bank[4][:, t * NE:(t + 1) * NE],
                                [v[:, kt, t // 4, (t % 4) * P:(t % 4 + 1) * P] for v in xt_hl],
                                [rw[:, u, kt, :] for u in range(2)], kt == 0, kt == KT - 1)
            r.then_inc(rt_full, 1)
            for st in ffn:
                if st[0] == "h":
                    p = st[1]
                    tb, k = pairs[p]
                    if p >= 2:
                        tb2, k2 = pairs[p - 2]
                        if k2 < 4:
                            pe.wait_ge(h_free[p % 2], shared_before(pairs, p - 2))
                        else:
                            pe.wait_ge(g_ready, entry_of_pair(p - 2) + 2)
                    if k < 4:
                        if k == 0 and tb == 0:
                            pe.wait_ge(w_split, NSW)
                        rhs = lambda kt: [v[:, kt, tb, :] for v in xt_hl]
                        for i in range(2):
                            for kt in range(KT):
                                w = SWH[:, 2 * i + kt, :]
                                r = product(bank[2 * (p % 2) + i][:, :],
                                            [w[:, u * N + k * P:u * N + (k + 1) * P] for u in range(2)],
                                            rhs(kt), kt == 0, kt == KT - 1)
                    else:
                        q = tb * NE + k - 4
                        pe.wait_ge(w_split, NSW + 2 * q + 2)
                        for i in range(2):
                            for kt in range(KT):
                                c0 = kt * D + i * P
                                r = product(bank[2 * (p % 2) + i][:, :],
                                            [R1[:, (2 * q) % 8, u * N + c0:u * N + c0 + P] for u in range(2)],
                                            [v[:, kt, tb, :] for v in xt_hl], kt == 0, kt == KT - 1)
                    r.then_inc(h_full, 1)
                else:
                    y = st[1]
                    tb, k = y // (NE + 1), y % (NE + 1)
                    if y == 0:
                        pe.wait_ge(rt_exp, 1)
                    if y >= 2:
                        pe.wait_ge(y_free, y - 1)
                    ents = [tb * (4 + 2 * NE) + i for i in (range(4) if k == 0 else (2 + 2 * k, 3 + 2 * k))]
                    pe.wait_ge(ht_ready, ents[-1] + 1)
                    for t in range(4):
                        o = bank[4 + 2 * (y % 2) + t // 2][:, (t % 2) * D:(t % 2 + 1) * D]
                        for i, e in enumerate(ents):
                            lhs = [WH[:, 2 * (e % HR) + u, t * P:(t + 1) * P] for u in range(2)]
                            if k == 0:
                                w, c0 = SWH[:, 4 + i // 2, :], (i % 2) * D
                            else:
                                w, c0 = R1[:, (2 * (tb * NE + k - 1) + 1) % 8, :], i * D
                            r = product(o, lhs, [w[:, u * N + c0:u * N + c0 + D] for u in range(2)],
                                        i == 0, i == len(ents) - 1)
                    r.then_inc(y_full, 1)


def raw(ap):
    return ap.bitcast(F32)


def shared_before(pairs, p):
    return sum(1 for i in range(p + 1) if i % 2 == p % 2 and pairs[i][1] < 4)


_OUTS = [((1024, 256), 'float32')]


def kernel(**inputs):
    import numpy as _np
    import concourse.bacc as _bacc
    from concourse import mybir as _mybir
    from concourse.bass_utils import run_bass_kernel_spmd as _run

    nc = _bacc.Bacc("TRN2", target_bir_lowering=False, num_devices=1)
    a = {k: _np.asarray(v) for k, v in inputs.items()}
    data = {
        "x": a["x"].reshape(B * S, D),
        "ctxT": a["ctx_1024"].reshape(B * T, D).T,
        "bqkT": _np.stack([a["L0_xattn_b_Q"], a["L0_xattn_b_K"]]).reshape(2 * KT, P).T,
        "wqT": a["L0_xattn_W_Q"].T, "wkT": a["L0_xattn_W_K"].T,
        "wvT": a["L0_xattn_W_V"].T, "bv": a["L0_xattn_b_V"],
        "woT": a["L0_xattn_W_O"].T, "bo": a["L0_xattn_b_O"],
        "rwT": a["L0_ffn_router_w"].T, "rbias": a["L0_ffn_router_bias"],
        "sw1": a["L0_ffn_sw1"], "sw3": a["L0_ffn_sw3"], "sw2": a["L0_ffn_sw2"],
        "ew1": a["L0_ffn_ew1"], "ew2": a["L0_ffn_ew2"],
    }
    arrays, args = {}, []
    for name, v in data.items():
        v = _np.ascontiguousarray(v)
        arrays[f"in_{name}_dram"] = v
        args.append(nc.dram_tensor(f"in_{name}_dram", v.shape, _mybir.dt.from_np(v.dtype), kind="ExternalInput").ap())
    args.append(nc.dram_tensor("out_0_dram", (B * S, D), F32, kind="ExternalOutput").ap())
    xattn_ffn(nc, *args)
    r = _run(nc, [arrays], core_ids=[0])
    return r.results[0]["out_0_dram"].reshape(B, S, D)
```

```python
from contextlib import ExitStack

import concourse.bass as bass
from concourse import mybir

F32 = mybir.dt.float32
F32R = mybir.dt.float32r
BF16 = mybir.dt.bfloat16
ALU = mybir.AluOpType
ACT = mybir.ActivationFunctionType
AX = mybir.AxisListType

P = 128
B, S, T, D = 2, 512, 1024, 256
NH, DK = 16, 16
NE, HS = 8, 512
N = 512
KT = D // P
GH = 4
NG = B * NH // GH
HG = NH // GH
QT = S // P
KP = T // P // 2
UG = GH * KP
NU = NG * UG
LEAD = 20
TERMS = 6
KROWS = TERMS * DK
EPS = 1e-5
SLOTS = 3
PR = 8
HR = 7
EW = 6


def xattn_ffn(nc, x, ctxT, wqT, wkT, wvT, woP, smalls, bias_rows, sw1, sw3, sw2, ew1, ew2, out):
    splits = [("w", 0), ("c", 0, 0), ("c", 0, 1), ("w", 1), ("w", 2), ("c", 1, 0), ("c", 1, 1)]
    NSP = len(splits)
    jobs = [("K", 0, 0, 0), ("K", 0, 0, 1), ("T", 0, 0, 0), ("T", 0, 1, 0), ("Q", 0, 0, 0),
            ("K", 0, 1, 0), ("K", 0, 1, 1), ("Q", 0, 1, 0)] + [("V", 0, i, 0) for i in range(4)]
    jobs += [("T", 1, 0, 0), ("T", 1, 1, 0)]
    for m in range(2):
        jobs += [("K", 1, m, 0), ("K", 1, m, 1), ("Q", 1, m, 0)]
    jobs += [("V", 1, i, 0) for i in range(4)] + [("B", 0, 0, 0)]
    NJ = len(jobs)
    kq_jobs = [j for j in jobs if j[0] in "KQ"]
    kq_of = {j: c for c, j in enumerate(kq_jobs)}

    def job_frees(i, upto):
        return sum(1 for n in range(upto) if n % 4 == i)

    def around_unit(n):
        todo = []
        m = n + LEAD
        if m < NU:
            todo += [("max", m)]
        g1 = (m - UG - 1) // UG
        if (m - UG - 1) % UG == 0 and 0 < g1 < NG:
            todo += [("negmax", g1)]
        if n % 2 == 1 and n >= 5:
            q = n // 4 - 1
            if q < NU // 4:
                todo += [("pv", q, (n % 4) // 2)]
        g, r = n // UG - 1, n % UG
        if 0 <= g < NG:
            if r == 3:
                todo += [("evac", g)]
            if r == 5:
                todo += [("recip", g)]
            if g < NG - 1:
                if r == 9:
                    todo += [("sums", g)]
                if r == 11:
                    todo += [("norm", g)]
                if r == 14 and g % HG == HG - 1:
                    todo += [("oproj", g // HG)]
        if n == 6 * UG + 2:
            todo += [("ln2", 0)]
        if n == 6 * UG + 8:
            todo += [("xpose2", 0)]
        if n == 6 * UG + 13:
            todo += [("router", 0)]
        return todo

    steps = [("split", i) for i in range(3)] + [("stats", 0), ("job", 0), ("job", 1), ("mid", 0), ("norm1", 0)]
    steps += [("split", 3), ("mid", 1), ("job", 2), ("job", 3), ("mid", 2), ("mid", 3), ("job", 4), ("split", 4)]
    steps += [("job", 5), ("mid", 4), ("norm1", 1), ("job", 6), ("mid", 5), ("split", 5), ("job", 7), ("mid", 6)]
    steps += [("split", 6), ("mid", 7)]
    m = 0
    for n in range(8, NJ):
        steps.append(("job", n))
        if m < UG and n >= 9:
            steps.append(("max", m))
            m += 1
        if n > 8:
            steps.append(("mid", n - 1))
    steps += [("mid", NJ - 1), ("clear",)] + [("max", i) for i in range(m, UG)]
    steps += [("negmax", 0)] + [("max", m) for m in range(UG, LEAD)]
    for n in range(NU + 6):
        if n < NU:
            steps.append(("unit", n))
        steps += around_unit(n)

    pairs = [(tb, k) for tb in range(2) for k in range(4 + NE)]
    steps += [("h", 0), ("h", 1), ("sums", NG - 1), ("norm", NG - 1), ("h", 2), ("h", 3), ("oproj", 1)]
    for p in range(4, len(pairs)):
        tb, k = pairs[p]
        if p == 5:
            steps.append(("ln2", 1))
        steps.append(("h", p))
        if p == 6:
            steps += [("xpose2", 1), ("router", 1)]
        if k == 4:
            steps.append(("y", tb * (NE + 1)))
        elif k > 4:
            steps.append(("y", tb * (NE + 1) + k - 4))
        elif k == 0:
            steps.append(("y", tb * (NE + 1) - 1))
    steps.append(("y", 2 * (NE + 1) - 1))

    ring_at = {}
    for st in steps:
        if st[0] in ("max", "negmax", "sums", "oproj", "xpose2", "router", "y"):
            ring_at[st] = len(ring_at)

    def y_of_entry(i):
        tb, k = i // (4 + 2 * NE), i % (4 + 2 * NE)
        return tb * (NE + 1) + (0 if k < 4 else 1 + (k - 4) // 2)

    def entry_of_pair(p):
        tb, k = pairs[p]
        return tb * (4 + 2 * NE) + (k if k < 4 else 4 + 2 * (k - 4))

    NSW = 6
    NCH = NSW + 2 * 2 * NE
    sw_src = [sw1[0:P, :], sw1[P:D, :], sw3[0:P, :], sw3[P:D, :],
              sw2[0:2 * P, :].rearrange("(k p) n -> p k n", p=P), sw2[2 * P:, :].rearrange("(k p) n -> p k n", p=P)]
    EARLY = NSW + EW

    def chunk_src(c):
        if c < NSW:
            return sw_src[c]
        q = (c - NSW) // 2 % NE
        return (ew1, ew2)[(c - NSW) % 2][q].rearrange("(k p) n -> p k n", p=P)

    with ExitStack() as ctx:
        def sb(name, shape, dt):
            return ctx.enter_context(nc.sbuf_tensor(name, shape, dt))

        def sem(name):
            return ctx.enter_context(nc.semaphore(name))

        psum = ctx.enter_context(nc.psum_tensor("psum", [P, 8, N], F32))
        bank = [psum[:, i, :] for i in range(8)]
        acc = bank[3]

        x_sb = sb("x_sb", [P, 8, D], F32)
        R1 = sb("R1", [P, 8, 1024], F32R)
        SWH = sb("SWH", [P, NSW, 1024], F32R)
        WH = sb("WH", [P, 10, N], F32R)
        XT = sb("XT", [P, 8, N], F32R)
        PB = sb("PB", [P, PR, 2 * N], F32)
        VA = sb("VA", [P, B, 8, NH, DK + 1], F32)
        QS = [sb(f"QS{i}", [P, GH, S], BF16) for i in range(SLOTS)]
        KS = [sb(f"KS{i}", [P, GH, T], BF16) for i in range(SLOTS)]
        RAW = sb("RAW", [P, 2, N], F32)
        TMP = sb("TMP", [P, 4, N], F32)
        PARTS = sb("PARTS", [P, 2, 3, N], BF16)
        parts = [PARTS[:, 0], PARTS[:, 1],
                 RAW[:, :, :].bitcast(BF16).rearrange("p a b -> p (a b)")[:, 0:3 * N].rearrange("p (i n) -> p i n", i=3)]
        small = sb("small", [P, 4 + HG + KT * NE], F32)
        bqk, bv_sb = small[:, 0:4], small[:, 4:4 + HG]
        rw_raw = small[:, 4 + HG:].rearrange("p (k e) -> p k e", k=KT)
        rows = sb("rows", [P, D + NE], F32)
        bo_sb, rb_sb = rows[:, 0:D], rows[:, D:]
        rw = sb("rw", [P, 2, KT, NE], F32R)
        ident = sb("ident", [P, P], F32)
        identb = sb("identb", [P, P], BF16)
        sel = sb("sel", [P, P], F32)
        stats = sb("stats", [P, 8, 6], F32)
        mv = sb("mv", [P, 8, 2], F32)
        ve = sb("ve", [P, 8], F32)
        lnv = sb("lnv", [P, 8], F32)
        rstd0 = sb("rstd0", [P, 8], F32)
        nt1 = sb("nt1", [P, 8], F32)
        nt2 = sb("nt2", [P, 8], F32)
        rstd = sb("rstd", [P, 8], F32)
        negm = sb("negm", [P, 2, GH, QT], F32)
        nhl = sb("nhl", [P, 2, QT, 2, GH], BF16)
        one8 = sb("one8", [P, 4 * NE], F32)
        rs = sb("rs", [P, 8, 8], F32)
        desc = sb("desc", [P, NE], F32)
        comb = sb("comb", [P, 8, NE], F32)

        sums16 = sb("sums16", [P, GH * N // P], F32)
        rsum16 = sb("rsum16", [P, GH * N // P], F32)
        xn = KS[2][:, :, :].bitcast(F32).rearrange("p a b -> p (a b)").rearrange("p (t d) -> p t d", d=D)
        craw = PB[:, 0:4, :].rearrange("p a b -> p (a b)").rearrange("p (k t) -> p k t", k=KT)
        wraw = PB[:, 4:6, :].rearrange("p a b -> p (a b)").rearrange("p (w k n) -> p w k n", w=4, k=KT)
        woraw = PB[:, 6, :].rearrange("p (g n) -> p g n", g=HG)
        R1f = R1[:, :, :].rearrange("p a b -> p (a b)")
        ctx_hl = [R1f[:, i * 4096:(i + 1) * 4096].rearrange("p (k t) -> p k t", k=KT) for i in range(2)]
        w_hl = [[WH[:, 2 * w + i, :].rearrange("p (k n) -> p k n", k=KT) for i in range(2)] for w in range(3)]
        WK, WQ, WV = 0, 1, 2
        wo_hl = [WH[:, 6 + 2 * i:8 + 2 * i, :].rearrange("p a b -> p (a b)").rearrange("p (g n) -> p g n", g=HG)
                 for i in range(2)]
        xt_hl = [XT[:, 4 * i:4 * i + 4, :].rearrange("p (k b) n -> p k b n", b=2) for i in range(2)]
        U, RC, RU = TMP[:, 0, :], TMP[:, 1, :], TMP[:, 3, :]
        ao = [[WH[:, 2 * i + u, :] for u in range(2)] for i in range(3)] + [[XT[:, 1, :], XT[:, 3, :]]]
        hid = [[R1[:, 6 + i, u * N:(u + 1) * N] for u in range(2)] for i in range(2)]
        hid += [[WH[:, 2 * i + u, :] for u in range(2)] for i in range(5)]
        nrow = TMP[0:2 * GH, 2, :].bitcast(BF16).rearrange("p (b n) -> p b n", b=2)
        rt = QS[2][:, :, :].bitcast(F32).rearrange("p a b -> p (a b)")[:, 0:12 * 8 * NE]\
            .rearrange("p (i t e) -> p i t e", i=12, e=NE)

        qs_d = nc.dram_tensor("qs_d", (B, 2, 3, 2, DK, GH, S), BF16, kind="Internal").ap()
        ks_d = nc.dram_tensor("ks_d", (B, 2, 3, 2, DK, GH, T), BF16, kind="Internal").ap()

        ld_x = sem("ld_x")
        ld_ctx = [sem(f"ld_ctx{i}") for i in range(3)]
        ld_w = [sem(f"ld_w{w}") for w in range(3)]
        ld_wo = sem("ld_wo")
        ld_small = sem("ld_small")
        ld_rows = sem("ld_rows")
        consts = sem("consts")
        const_step = sem("const_step")
        ones2 = sem("ones2")
        acc_zero = sem("acc_zero")
        var_ready = sem("var_ready")
        rstd_guess = sem("rstd_guess")
        act_chain = sem("act_chain")
        dve_chain = sem("dve_chain")
        xn_ready = sem("xn_ready")
        split_hi = sem("split_hi")
        split_lo = sem("split_lo")
        pool_split = sem("pool_split")
        pool_chain = sem("pool_chain")
        jobs_done = sem("jobs_done")
        job_free = [sem(f"job_free{i}") for i in range(4)]
        xt_hi = sem("xt_hi")
        kq_hi = sem("kq_hi")
        kq_mid = sem("kq_mid")
        kq_split = sem("kq_split")
        kq_stored = [sem(f"kq_stored{c}") for c in range(len(kq_jobs))]
        stk_loaded = [sem(f"stk_loaded{i}") for i in range(SLOTS)]
        bias_loaded = [sem(f"bias_loaded{i}") for i in range(2)]
        ring_full = sem("ring_full")
        ring_empty = sem("ring_empty")
        negm_ready = sem("negm_ready")
        scores_done = sem("scores_done")
        exp_done = sem("exp_done")
        pv_done = sem("pv_done")
        u_ready = sem("u_ready")
        a_hi = sem("a_hi")
        a_lo = sem("a_lo")
        bo_added = sem("bo_added")
        wraw_loaded = [sem(f"wraw_loaded{i}") for i in range(2)]
        w_split = sem("w_split")
        t2_hi = sem("t2_hi")
        rt_logits = sem("rt_logits")
        su_loaded = sem("su_loaded")
        su_recip = sem("su_recip")
        ru_loaded = sem("ru_loaded")
        ru_zero = sem("ru_zero")
        rt_exp = sem("rt_exp")
        h_full = sem("h_full")
        h_free = [sem(f"h_free{i}") for i in range(2)]
        g_ready = sem("g_ready")
        ht_ready = sem("ht_ready")
        stored = sem("stored")

        block = ctx.enter_context(nc.Block())

        def ring_bank(st, i=0):
            return bank[4 + 2 * (ring_at[st] % 2) + i]

        def kq_count(b, m):
            return 3 * (2 * b + m)

        @block.sync
        def _(sp):
            cT = ctxT.rearrange("(k p) t -> p k t", p=P)
            sp.dma_start(wraw[:, WK], wkT.rearrange("(k p) n -> p k n", p=P)).then_inc(ld_w[WK], 16)
            for tb in range(2):
                sp.dma_start(craw[:, :, tb * N:(tb + 1) * N], cT[:, :, tb * N:(tb + 1) * N]).then_inc(ld_ctx[tb], 16)
            sp.dma_start(x_sb[:, :, :], x.rearrange("(t p) d -> p t d", p=P)).then_inc(ld_x, 16)
            sp.dma_start(wraw[:, WQ], wqT.rearrange("(k p) n -> p k n", p=P)).then_inc(ld_w[WQ], 16)
            sp.dma_start(wraw[:, WV], wvT.rearrange("(k p) n -> p k n", p=P)).then_inc(ld_w[WV], 16)
            sp.dma_start(craw[:, :, T:], cT[:, :, T:]).then_inc(ld_ctx[2], 16)

            def load_stack(g):
                b, hg, s = g // HG, g % HG, g % SLOTS
                if hg % 2 == 0:
                    for c in range(kq_count(b, hg // 2), kq_count(b, hg // 2) + 3):
                        sp.wait_ge(kq_stored[c], 16)
                if g == 2:
                    sp.wait_ge(jobs_done, jobs.index(("T", 1, 1, 0)) + 1)
                if g >= SLOTS:
                    sp.wait_ge(scores_done, 2 * UG * (g - SLOTS + 1))
                row = 0
                for n in (3, 2, 1):
                    rows = slice(row, row + n * DK)
                    sp.dma_start(QS[s][rows, :, :].rearrange("r j t -> r (j t)"),
                                 qs_d[b, hg // 2, 3 - n:4 - n, hg % 2].rearrange("o d j t -> o d (j t)")
                                 .broadcast_to([n, DK, GH * S])).then_inc(stk_loaded[s], 16)
                    sp.dma_start(KS[s][rows, :, :].rearrange("r j t -> r (j t)"),
                                 ks_d[b, hg // 2, 0:n, hg % 2].rearrange("p d j t -> p d (j t)"))\
                        .then_inc(stk_loaded[s], 16)
                    row += n * DK

            def load_bias(g):
                sp.wait_ge(ring_empty, ring_at[("negmax", g)] + 1)
                for c in range(2):
                    sp.dma_start(QS[g % SLOTS][KROWS + c:KROWS + c + 1, :, :],
                                 nrow[GH * c:GH * c + GH, g % 2, :]).then_inc(bias_loaded[g % 2], 16)

            def load_chunk(c):
                if c == 0:
                    sp.wait_ge(kq_stored[11], 16)
                if c >= 2:
                    sp.wait_ge(w_split, c - 1)
                dst = RAW[:, c % 2, :]
                if c >= 4:
                    dst = dst.rearrange("p (k n) -> p k n", k=2)
                sp.dma_start(dst, chunk_src(c)).then_inc(wraw_loaded[c % 2], 16)

            for c, (kind, b, m, tb) in enumerate(kq_jobs):
                sp.wait_ge(kq_split, c + 1)
                dst = qs_d[b, m] if kind == "Q" else ks_d[b, m, :, :, :, :, tb * N:(tb + 1) * N]
                sp.dma_start(dst.rearrange("p l d j t -> (l d j) p t"), parts[c % 3])\
                    .then_inc(kq_stored[c], 16)
                if c == 2:
                    load_stack(0)
                if c == 4:
                    load_stack(1)
                if c == 8:
                    load_stack(2)
            load_bias(0)
            for g in range(NG):
                if g + 1 < NG:
                    load_bias(g + 1)
                if g + SLOTS < NG:
                    load_stack(g + SLOTS)
                sp.wait_ge(u_ready, g + 1)
                sp.dma_start(sums16[:, :], U[DK::32, :]).then_inc(su_loaded, 16)
                sp.wait_ge(su_recip, g + 1)
                sp.dma_start(RU[DK::32, :], rsum16[:, :]).then_inc(ru_loaded, 16)
                for c in range(2 * g, min(2 * g + 2, EARLY)):
                    load_chunk(c)
            for c in range(EARLY, NCH):
                load_chunk(c)
            for tb in range(2):
                sp.wait_ge(ring_empty, ring_at[("y", (tb + 1) * (NE + 1) - 1)] + 1)
                sp.dma_start(out.rearrange("(t p) d -> p t d", p=P)[:, 4 * tb:4 * tb + 4, :],
                             x_sb[:, 4 * tb:4 * tb + 4, :]).then_inc(stored, 16)
            sp.wait_ge(stored, 32)

        @block.gpsimd
        def _(pool):
            k = 0
            for t in (ident, identb, sel):
                pool.memset(t[:, :], 0.0).then_inc(const_step, 1)
            pool.memset(RU, 0.0).then_inc(ru_zero, 1)
            pool.memset(VA[:, :, :, :, DK:DK + 1], 1.0).then_inc(consts, 1)
            for e in range(NE):
                pool.memset(desc[:, e:e + 1], float(NE - e)).then_inc(consts, 1)
            pool.wait_ge(const_step, 3)
            for t in (ident, identb):
                pool.affine_select(out=t[:, :], in_=t[:, :], compare_op=ALU.not_equal, fill=1.0, base=0,
                                   pattern=[[-1, P]], channel_multiplier=1).then_inc(consts, 1)
            sv = sel[:, :].rearrange("p (a i) -> p a i", a=4)
            pool.affine_select(out=sv, in_=sv, compare_op=ALU.not_equal, fill=1.0, base=-DK,
                               pattern=[[-32, 4], [0, 32]], channel_multiplier=1).then_inc(consts, 1)

            pool.wait_ge(consts, 1 + NE + 3)
            for s in range(2):
                pool.memset(KS[s][KROWS:KROWS + 2, :, :], 1.0).then_inc(consts, 1)
                pool.wait_ge(consts, 1 + NE + 3 + s + 1)

            pool.wait_ge(ld_small, 16)
            pool.tensor_scalar(rw[:, 0], rw_raw, 1.0, 1.0, ALU.mult, ALU.mult).then_inc(pool_chain, 1)
            pool.wait_ge(ld_wo, 16)
            pool.tensor_scalar(wo_hl[0], woraw, 1.0, 1.0, ALU.mult, ALU.mult).then_inc(pool_chain, 1)
            pool.wait_ge(pool_chain, 2)
            pool.tensor_tensor(rw[:, 1], rw_raw, raw(rw[:, 0]), ALU.subtract).then_inc(pool_split, 1)
            pool.tensor_tensor(wo_hl[1], woraw, raw(wo_hl[0]), ALU.subtract).then_inc(pool_split, 1)

            for c in range(len(kq_jobs)):
                pool.wait_ge(kq_mid, c + 1)
                pool.tensor_tensor(parts[c % 3][:, 2, :], TMP[:, c % 3, :], parts[c % 3][:, 1, :], ALU.subtract)\
                    .then_inc(kq_split, 1)
            pool.wait_ge(jobs_done, jobs.index(("T", 1, 1, 0)) + 1)
            pool.wait_ge(kq_split, len(kq_jobs))
            pool.memset(KS[2][KROWS:KROWS + 2, :, :], 1.0).then_inc(ones2, 1)
            pool.wait_ge(ones2, 1)
            pool.wait_ge(xn_ready, 8)
            pool.wait_ge(job_free[(NJ - 1) % 4], job_frees((NJ - 1) % 4, NJ))
            for t in range(8):
                pool.tensor_tensor(x_sb[:, t, :], x_sb[:, t, :], bo_sb[:, :], ALU.add).then_inc(bo_added, 1)

            def split_chunk(c):
                pool.wait_ge(wraw_loaded[c % 2], 16 * (c // 2 + 1))
                if c < NSW:
                    hi, lo = SWH[:, c, 0:N], SWH[:, c, N:]
                else:
                    s = (c - NSW) % EW
                    hi, lo = R1[:, s, 0:N], R1[:, s, N:]
                    if c == NSW:
                        pool.wait_ge(jobs_done, NJ)
                    if c >= EARLY:
                        q = (c - EARLY) // 2
                        pool.wait_ge(ring_full, ring_at[("y", q // NE * (NE + 1) + 1 + q % NE)] + 1)
                pool.tensor_scalar(hi, RAW[:, c % 2, :], 1.0, 1.0, ALU.mult, ALU.mult).then_inc(pool_chain, 1)
                pool.wait_ge(pool_chain, 3 + c)
                pool.tensor_tensor(lo, RAW[:, c % 2, :], raw(hi), ALU.subtract).then_inc(w_split, 1)

            for g in range(NG):
                for c in range(2 * g, min(2 * g + 2, EARLY)):
                    split_chunk(c)
                pool.wait_ge(a_hi, g + 1)
                pool.tensor_tensor(ao[g % HG][1], RC, raw(ao[g % HG][0]), ALU.subtract).then_inc(a_lo, 1)
            for c in range(EARLY, NCH):
                split_chunk(c)

        @block.scalar
        def _(act):
            chain = [0]

            def link(ins):
                chain[0] += 1
                ins.then_inc(act_chain, 1)
                act.wait_ge(act_chain, chain[0])

            act.dma_start(small[:, :], smalls).then_inc(ld_small, 16)
            act.dma_start(woraw, woP).then_inc(ld_wo, 16)
            act.dma_start(rows[:, :], bias_rows.rearrange("(a n) -> a n", a=1).broadcast_to([P, D + NE]))\
               .then_inc(ld_rows, 16)

            def first_rstd(n):
                act.wait_ge(var_ready, n)
                link(act.activation(lnv[:, :], ve[:, :], ACT.Ln))
                act.activation(rstd0[:, :], lnv[:, :], ACT.Exp, scale=-0.5).then_inc(rstd_guess, 1)

            def split_high(i):
                it = splits[i]
                if it[0] == "w":
                    act.wait_ge(ld_w[it[1]], 16)
                    act.activation(w_hl[it[1]][0], wraw[:, it[1]], ACT.Copy).then_inc(split_hi, 1)
                else:
                    act.wait_ge(ld_ctx[it[2] if it[1] == 0 else 2], 16)
                    c0 = it[1] * T + it[2] * N
                    act.activation(ctx_hl[0][:, :, c0:c0 + N], craw[:, :, c0:c0 + N], ACT.Copy).then_inc(split_hi, 1)

            def job(n):
                kind, b, m, tb = jobs[n]
                if kind == "T":
                    act.wait_ge(jobs_done, n + 1)
                    act.activation(xt_hl[0][:, m, b, :], bank[n % 4][:, :], ACT.Copy).then_inc(xt_hi, 1)
                if kind == "V":
                    act.wait_ge(jobs_done, n + 1)
                    act.activation(VA[:, b, 2 * m:2 * m + 2, :, 0:DK],
                                   bank[n % 4].rearrange("p (t h d) -> p t h d", t=2, h=NH), ACT.Copy)\
                       .then_inc(job_free[n % 4], 1)
                if kind in "KQ":
                    c = kq_of[jobs[n]]
                    act.wait_ge(jobs_done, n + 1)
                    if c == 0:
                        act.wait_ge(ld_small, 16)
                    if c >= 3:
                        act.wait_ge(kq_split, c - 2)
                        act.wait_ge(kq_stored[c - 3], 16)
                    bias = bqk[:, m:m + 1] if kind == "Q" else bqk[:, 2 + m:3 + m]
                    act.activation(TMP[:, c % 3, :], bank[n % 4][:, :], ACT.Identity, bias=bias).then_inc(kq_hi, 1)
                    act.activation(parts[c % 3][:, 0, :], bank[n % 4][:, :], ACT.Identity, bias=bias)\
                        .then_inc(job_free[n % 4], 1)

            def unit(n):
                if n >= PR:
                    act.wait_ge(pv_done, 2 * (n // 4) - 2)
                elif n == 0:
                    act.wait_ge(pool_split, 2)
                    act.wait_ge(split_lo, NSP)
                for i in range(2):
                    act.wait_ge(scores_done, 2 * n + i + 1)
                    act.activation(PB[:, n % PR, i * N:(i + 1) * N], bank[(2 * n + i) % 3], ACT.Exp,
                                   scale=DK ** -0.5).then_inc(exp_done, 1)

            def hidden(p):
                tb, k = pairs[p]
                act.wait_ge(h_full, p + 1)
                if p == 0:
                    act.wait_ge(pv_done, 2 * (NU // 4 - 1))
                for i in range(1 if k < 4 else 2):
                    e = entry_of_pair(p) + i
                    if e >= 4:
                        act.wait_ge(ht_ready, e - 3)
                    act.activation(PB[:, e % 4, N:], bank[2 * (p % 2) + i], ACT.Silu if k < 4 else ACT.Gelu)\
                       .then_inc(g_ready, 1)

            rstds = 0
            for st in steps:
                if st[0] == "split":
                    split_high(st[1])
                elif st[0] == "job":
                    job(st[1])
                elif st[0] in ("stats", "ln2"):
                    rstds += 1
                    first_rstd(rstds)
                elif st[0] == "unit":
                    unit(st[1])
                elif st[0] == "evac":
                    g = st[1]
                    act.wait_ge(pv_done, 2 * (g + 1) * KP)
                    if g:
                        act.wait_ge(ring_empty, ring_at[("sums", g - 1)] + 1)
                    else:
                        act.wait_ge(kq_split, len(kq_jobs))
                        act.wait_ge(acc_zero, 1)
                    act.activation(U, acc, ACT.Copy).then_inc(u_ready, 1)
                elif st[0] == "norm":
                    g = st[1]
                    act.wait_ge(ring_empty, ring_at[("sums", g)] + 1)
                    if g == 0:
                        act.wait_ge(jobs_done, NJ)
                    if g == HG:
                        act.wait_ge(ring_full, ring_at[("oproj", 0)] + 1)
                    act.activation(ao[g % HG][0], RC, ACT.Copy).then_inc(a_hi, 1)
                elif st[0] == "xpose2":
                    b = st[1]
                    act.wait_ge(ring_full, ring_at[st] + 1)
                    for i in range(2):
                        act.activation(xt_hl[0][:, i, b, :], ring_bank(st, i), ACT.Copy).then_inc(t2_hi, 1)
                elif st[0] == "router":
                    b = st[1]
                    act.wait_ge(rt_logits, b + 1)
                    act.activation(rt[:, 1, 4 * b:4 * b + 4], rt[:, 0, 4 * b:4 * b + 4], ACT.Exp, scale=-1.0)\
                       .then_inc(rt_exp, 1)
                elif st[0] == "h":
                    hidden(st[1])

        @block.vector
        def _(dve):
            chain = [0]

            def link(ins):
                chain[0] += 1
                ins.then_inc(dve_chain, 1)
                dve.wait_ge(dve_chain, chain[0])


            def layer_stats(n, tiles):
                for t in tiles:
                    last = dve.bn_stats(stats[:, t, :], x_sb[:, t, :])
                link(last)
                for t in tiles:
                    last = dve.bn_aggr(mv[:, t, :], stats[:, t, :])
                link(last)
                dve.tensor_scalar(ve[:, :], mv[:, :, 1], EPS, None, ALU.add).then_inc(var_ready, 1)

            def refine_rstd(n):
                dve.wait_ge(rstd_guess, n)
                link(dve.tensor_tensor(nt1[:, :], rstd0[:, :], rstd0[:, :], ALU.mult))
                link(dve.tensor_tensor(nt2[:, :], nt1[:, :], ve[:, :], ALU.mult))
                link(dve.tensor_scalar(nt1[:, :], nt2[:, :], -0.5, 1.5, ALU.mult, ALU.add))
                link(dve.tensor_tensor(rstd[:, :], rstd0[:, :], nt1[:, :], ALU.mult))

            def normalise(t):
                dve.tensor_scalar(xn[:, t, :], x_sb[:, t, :], mv[:, t, 0:1], rstd[:, t:t + 1],
                                  ALU.subtract, ALU.mult).then_inc(xn_ready, 1)

            def split_low(i):
                it = splits[i]
                dve.wait_ge(split_hi, i + 1)
                if it[0] == "w":
                    dve.tensor_tensor(w_hl[it[1]][1], wraw[:, it[1]], raw(w_hl[it[1]][0]), ALU.subtract)\
                        .then_inc(split_lo, 1)
                else:
                    c0 = it[1] * T + it[2] * N
                    dve.tensor_tensor(ctx_hl[1][:, :, c0:c0 + N], craw[:, :, c0:c0 + N],
                                      raw(ctx_hl[0][:, :, c0:c0 + N]), ALU.subtract).then_inc(split_lo, 1)

            def job(n):
                kind, b, m, tb = jobs[n]
                if kind == "T":
                    i = 2 * b + m
                    dve.wait_ge(xt_hi, i + 1)
                    dve.tensor_tensor(xt_hl[1][:, m, b, :], bank[n % 4][:, :], raw(xt_hl[0][:, m, b, :]), ALU.subtract)\
                        .then_inc(job_free[n % 4], 1)
                if kind in "KQ":
                    c = kq_of[jobs[n]]
                    dve.wait_ge(kq_hi, c + 1)
                    dve.wait_ge(job_free[n % 4], n // 4 + 1)
                    link(dve.tensor_tensor(TMP[:, c % 3, :], TMP[:, c % 3, :], parts[c % 3][:, 0, :], ALU.subtract))
                    dve.tensor_copy(parts[c % 3][:, 1, :], TMP[:, c % 3, :]).then_inc(kq_mid, 1)
                if kind == "B":
                    dve.wait_ge(jobs_done, n + 1)
                    dve.wait_ge(ld_rows, 16)
                    dve.tensor_tensor(bo_sb[:, :], bank[n % 4][:, 0:D], bo_sb[:, :], ALU.add)\
                       .then_inc(job_free[n % 4], 1)

            def route(st):
                b = st[1]
                ts = slice(4 * b, 4 * b + 4)
                (lg, e_, s_, sel_, eq, w_, oh, oh2, both, prod) = (rt[:, i, ts] for i in range(10))
                dst = comb[:, ts, :]
                if b == 0:
                    dve.wait_ge(consts, 14)
                    dve.wait_ge(ld_rows, 16)
                ring_wait(st)
                src = ring_bank(st)
                ins = dve.tensor_copy(lg, src[:, 0:4 * NE].rearrange("p (t e) -> p t e", e=NE))
                ins.then_inc(rt_logits, 1)
                dve.wait_ge(rt_logits, b + 1)
                dve.tensor_copy(rs[:, 0, 0:1], lg[:, 0, 0:1]).then_inc(ring_empty, 1)
                dve.wait_ge(rt_exp, b + 1)
                bc = lambda v: v.broadcast_to([P, 4, NE])
                col = lambda i: rs[:, i, ts].rearrange("p (t o) -> p t o", o=1)
                rbv = rb_sb[:, :].rearrange("p (o e) -> p o e", o=1)
                dsv = desc[:, :].rearrange("p (o e) -> p o e", o=1)
                link(dve.tensor_scalar(both, e_, 1.0, None, ALU.add))
                link(dve.reciprocal(s_, both))
                link(dve.tensor_tensor(sel_, s_, bc(rbv), ALU.add))

                def first_max(oh):
                    link(dve.tensor_reduce(col(0), sel_, AX.X, ALU.max))
                    link(dve.tensor_tensor(eq, sel_, bc(col(0)), ALU.is_equal))
                    link(dve.tensor_tensor(w_, eq, bc(dsv), ALU.mult))
                    link(dve.tensor_reduce(col(1), w_, AX.X, ALU.max))
                    link(dve.tensor_tensor(oh, w_, bc(col(1)), ALU.is_equal))

                first_max(oh)
                link(dve.scalar_tensor_tensor(out=sel_, in0=oh, scalar=-1e30, in1=sel_, op0=ALU.mult, op1=ALU.add))
                first_max(oh2)
                link(dve.tensor_tensor(both, oh, oh2, ALU.add))
                link(dve.tensor_tensor(prod, both, s_, ALU.mult))
                link(dve.tensor_reduce(col(4), prod, AX.X, ALU.add))
                link(dve.tensor_scalar(col(5), col(4), 1e-9, None, ALU.is_gt))
                link(dve.tensor_scalar(col(6), col(4), 1e-9, None, ALU.add))
                link(dve.reciprocal(col(7), col(6)))
                link(dve.tensor_tensor(col(6), col(7), col(5), ALU.mult))
                link(dve.tensor_scalar(col(7), col(5), -0.5, 0.5, ALU.mult, ALU.add))
                link(dve.tensor_tensor(prod, prod, bc(col(6)), ALU.mult))
                link(dve.tensor_tensor(both, both, bc(col(7)), ALU.mult))
                link(dve.tensor_tensor(dst, prod, both, ALU.add))

            def hidden(p):
                tb, k = pairs[p]
                for i in range(1 if k < 4 else 2):
                    e = entry_of_pair(p) + i
                    gt = PB[:, e % 4, N:]
                    hi, lo = hid[e % HR]
                    dve.wait_ge(g_ready, e + 1)
                    if k < 4:
                        dve.tensor_tensor(gt, gt, bank[2 * (p % 2) + 1], ALU.mult).then_inc(h_free[p % 2], 1)
                        dve.wait_ge(h_free[p % 2], shared_before(pairs, p))
                    if e >= HR:
                        dve.wait_ge(ring_full, ring_at[("y", y_of_entry(e - HR))] + 1)
                    elif e == 2:
                        dve.wait_ge(ring_full, ring_at[("oproj", 1)] + 1)
                    link(dve.tensor_copy(hi, gt))
                    dve.tensor_tensor(lo, gt, raw(hi), ALU.subtract).then_inc(ht_ready, 1)

            def add_y(y):
                tb, k = y // (NE + 1), y % (NE + 1)
                ring_wait(("y", y))
                for t in range(4):
                    src = ring_bank(("y", y), t // 2)[:, (t % 2) * D:(t % 2 + 1) * D]
                    dst = x_sb[:, 4 * tb + t, :]
                    if k == 0:
                        last = dve.tensor_tensor(dst, src, dst, ALU.add)
                    else:
                        last = dve.scalar_tensor_tensor(out=dst, in0=src, scalar=comb[:, 4 * tb + t, k - 1:k],
                                                        in1=dst, op0=ALU.mult, op1=ALU.add)
                last.then_inc(ring_empty, 1)
                dve.wait_ge(ring_empty, ring_at[("y", y)] + 1)

            def ring_wait(st):
                dve.wait_ge(ring_full, ring_at[st] + 1)

            def maxima(m):
                g, r = m // UG, m % UG
                ring_wait(("max", m))
                k0 = 4 + 2 * (ring_at[("max", m)] % 2)
                dve.tensor_reduce(negm[:, g % 2, r // QT, r % QT:r % QT + 1],
                                  psum[:, k0:k0 + 2, :].rearrange("p a n -> p (a n)"), AX.X, ALU.max, negate=True)\
                   .then_inc(ring_empty, 1)
                if r == UG - 1:
                    dve.wait_ge(ring_empty, ring_at[("max", m)] + 1)
                    nv = negm[:, g % 2].rearrange("p j q -> p q j")
                    link(dve.tensor_copy(nhl[:, g % 2, :, 0, :], nv))
                    dve.tensor_tensor(nhl[:, g % 2, :, 1, :], nv, nhl[:, g % 2, :, 0, :], ALU.subtract)\
                       .then_inc(negm_ready, 1)

            def xt_low(i, b, src):
                dve.wait_ge(t2_hi, 2 * b + i + 1)
                return dve.tensor_tensor(xt_hl[1][:, i, b, :], src, raw(xt_hl[0][:, i, b, :]), ALU.subtract)

            for st in steps:
                if st[0] == "mid":
                    job(st[1])
                elif st[0] == "clear":
                    dve.wait_ge(job_free[3], job_frees(3, NJ))
                    dve.memset(acc, 0.0).then_inc(acc_zero, 1)
                elif st[0] == "split":
                    split_low(st[1])
                elif st[0] == "stats":
                    dve.wait_ge(ld_x, 16)
                    layer_stats(1, range(8))
                elif st[0] == "norm1":
                    if st[1] == 0:
                        refine_rstd(1)
                    for t in range(4 * st[1], 4 * st[1] + 4):
                        normalise(t)
                elif st[0] == "ln2":
                    b = st[1]
                    if b == 0:
                        dve.wait_ge(scores_done, 2 * 6 * UG)
                    dve.wait_ge(ring_empty, ring_at[("oproj", b)] + 1)
                    layer_stats(2 + b, range(4 * b, 4 * b + 4))
                    refine_rstd(2 + b)
                    for t in range(4 * b, 4 * b + 4):
                        normalise(t)
                elif st[0] == "xpose2":
                    b = st[1]
                    ring_wait(st)
                    xt_low(0, b, ring_bank(st, 0))
                    xt_low(1, b, ring_bank(st, 1)).then_inc(ring_empty, 1)
                elif st[0] == "router":
                    route(st)
                elif st[0] == "max":
                    maxima(st[1])
                elif st[0] == "negmax":
                    g = st[1]
                    ring_wait(st)
                    src = ring_bank(st)
                    if g == 0:
                        dve.wait_ge(kq_split, len(kq_jobs))
                    if g >= 2:
                        dve.wait_ge(bias_loaded[g % 2], 32 * (g // 2))
                    dve.tensor_copy(nrow[:, g % 2, :], src[0:2 * GH, :]).then_inc(ring_empty, 1)
                elif st[0] == "sums":
                    g = st[1]
                    ring_wait(st)
                    src = ring_bank(st)
                    if g:
                        dve.wait_ge(a_lo, g)
                    dve.tensor_tensor(RC, src[:, :], U, ALU.mult).then_inc(ring_empty, 1)
                elif st[0] == "recip":
                    dve.wait_ge(su_loaded, 16 * (st[1] + 1))
                    if st[1]:
                        dve.wait_ge(ru_loaded, 16 * st[1])
                    dve.reciprocal(rsum16[:, :], sums16[:, :]).then_inc(su_recip, 1)
                elif st[0] == "oproj":
                    b = st[1]
                    dve.wait_ge(bo_added, 8)
                    ring_wait(st)
                    for i in range(2):
                        t = 4 * b + 2 * i
                        dst = x_sb[:, t:t + 2, :]
                        last = dve.tensor_tensor(dst, ring_bank(st, i).rearrange("p (t n) -> p t n", t=2), dst, ALU.add)
                    last.then_inc(ring_empty, 1)

                elif st[0] == "h":
                    hidden(st[1])
                elif st[0] == "y":
                    add_y(st[1])

        @block.tensor
        def _(pe):
            def product(dst, a_hl, b_hl, first=True, last=True):
                for i, (u, v) in enumerate(((0, 0), (0, 1), (1, 0))):
                    r = pe.matmul(dst, a_hl[u], b_hl[v], start=first and i == 0, stop=last and i == 2)
                return r

            def job(n):
                kind, b, m, tb = jobs[n]
                o = bank[n % 4]
                if n >= 4:
                    pe.wait_ge(job_free[n % 4], n // 4)
                if kind == "B":
                    pe.wait_ge(ld_small, 16)
                    pe.wait_ge(ld_wo, 16)
                    for hg in range(HG):
                        r = pe.matmul(o[:, 0:D], bv_sb[:, hg:hg + 1].broadcast_to([P, P]), woraw[:, hg, :],
                                      start=(hg == 0), stop=(hg == HG - 1))
                elif kind == "T":
                    pe.wait_ge(xn_ready, 4 * b + 4)
                    pe.wait_ge(consts, 14)
                    for t in range(4):
                        r = pe.transpose(o[:, t * P:(t + 1) * P], xn[:, 4 * b + t, m * P:(m + 1) * P], ident[:, :])
                elif kind == "K":
                    pe.wait_ge(split_lo, (2 + tb) if b == 0 else 6 + tb)
                    c0 = b * T + tb * N
                    for kt in range(KT):
                        r = product(o[:, :], [w[:, kt, m * P:(m + 1) * P] for w in w_hl[WK]],
                                    [c[:, kt, c0:c0 + N] for c in ctx_hl], kt == 0, kt == KT - 1)
                elif kind == "Q":
                    pe.wait_ge(split_lo, 4)
                    for kt in range(KT):
                        t = jobs.index(("T", b, kt, 0))
                        pe.wait_ge(job_free[t % 4], t // 4 + 1)
                    for kt in range(KT):
                        r = product(o[:, :], [w[:, kt, m * P:(m + 1) * P] for w in w_hl[WQ]],
                                    [t[:, kt, b, :] for t in xt_hl], kt == 0, kt == KT - 1)
                else:
                    pe.wait_ge(split_lo, 5 if b == 0 else 7)
                    for t in range(2):
                        c0 = b * T + (2 * m + t) * P
                        for kt in range(KT):
                            r = product(o[:, t * D:(t + 1) * D], [c[:, kt, c0:c0 + P] for c in ctx_hl],
                                        [w[:, kt, :] for w in w_hl[WV]], kt == 0, kt == KT - 1)
                r.then_inc(jobs_done, 1)

            def ring_wait(st):
                if ring_at[st] >= 2:
                    pe.wait_ge(ring_empty, ring_at[st] - 1)

            for st in steps:
                if st[0] == "job":
                    job(st[1])
                elif st[0] == "unit":
                    n = st[1]
                    g, r = n // UG, n % UG
                    kp, j = r // GH, r % GH
                    s = g % SLOTS
                    if r == 0:
                        pe.wait_ge(bias_loaded[g % 2], 32 * (g // 2 + 1))
                        if g == 2:
                            pe.wait_ge(ones2, 1)
                        pe.wait_ge(stk_loaded[s], 96 * (g // SLOTS + 1))
                    for i in range(2):
                        t = 2 * n + i
                        if t < 3:
                            pe.wait_ge(job_free[t], job_frees(t, NJ))
                        else:
                            pe.wait_ge(exp_done, t - 2)
                        k0 = (2 * kp + i) * P
                        pe.matmul(bank[t % 3], KS[s][0:KROWS + 2, j, k0:k0 + P], QS[s][0:KROWS + 2, j, :],
                                  start=True, stop=True).then_inc(scores_done, 1)
                elif st[0] == "max":
                    m = st[1]
                    g, r = m // UG, m % UG
                    s, j, qt = g % SLOTS, r // QT, r % QT
                    if r == 0:
                        pe.wait_ge(stk_loaded[s], 96 * (g // SLOTS + 1))
                    ring_wait(st)
                    for half in range(2):
                        last = pe.matmul(ring_bank(st, half), QS[s][0:KROWS, j, qt * P:(qt + 1) * P],
                                         KS[s][0:KROWS, j, half * N:(half + 1) * N], start=True, stop=True)
                    last.then_inc(ring_full, 1)
                elif st[0] == "negmax":
                    g = st[1]
                    ring_wait(st)
                    o = ring_bank(st)
                    pe.wait_ge(negm_ready, g + 1)
                    for qt in range(QT):
                        last = pe.matmul(o[0:2 * GH, qt * P:(qt + 1) * P],
                                         nhl[:, g % 2, qt].rearrange("p c j -> p (c j)"), identb[:, :],
                                         start=True, stop=True)
                    last.then_inc(ring_full, 1)
                elif st[0] == "pv":
                    q, kk = st[1:]
                    g, kp = q // KP, q % KP
                    if kk == 0:
                        pe.wait_ge(exp_done, 2 * (4 * q + 4))
                        if kp == 0:
                            if g:
                                pe.wait_ge(u_ready, g)
                            else:
                                pe.wait_ge(acc_zero, 1)
                    b, hg = g // HG, g % HG
                    for j in range(GH):
                        last = pe.matmul(acc[32 * j:32 * j + DK + 1, :], VA[:, b, 2 * kp + kk, GH * hg + j, :],
                                         PB[:, (4 * q + j) % PR, kk * N:(kk + 1) * N],
                                         start=(kp == 0 and kk == 0), stop=(kp == KP - 1 and kk == 1))
                    last.then_inc(pv_done, 1)
                elif st[0] == "sums":
                    g = st[1]
                    ring_wait(st)
                    o = ring_bank(st)
                    pe.wait_ge(ru_loaded, 16 * (g + 1))
                    pe.matmul(o[:, :], sel[:, :], RU, start=True, stop=True).then_inc(ring_full, 1)
                elif st[0] == "oproj":
                    b = st[1]
                    pe.wait_ge(a_lo, HG * (b + 1))
                    pe.wait_ge(pool_split, 2)
                    ring_wait(st)
                    for i in range(2):
                        o = ring_bank(st, i)
                        for t in range(2):
                            t0 = (2 * i + t) * P
                            for hg in range(HG):
                                last = product(o[:, t * D:(t + 1) * D], [a[:, t0:t0 + P] for a in ao[hg]],
                                               [w[:, hg, :] for w in wo_hl], hg == 0, hg == HG - 1)
                    last.then_inc(ring_full, 1)
                elif st[0] == "xpose2":
                    b = st[1]
                    pe.wait_ge(xn_ready, 8 + 4 * b + 4)
                    ring_wait(st)
                    for i in range(2):
                        for t in range(4):
                            r = pe.transpose(ring_bank(st, i)[:, t * P:(t + 1) * P],
                                             xn[:, 4 * b + t, i * P:(i + 1) * P], ident[:, :])
                    r.then_inc(ring_full, 1)
                elif st[0] == "router":
                    b = st[1]
                    pe.wait_ge(ring_empty, ring_at[("xpose2", b)] + 1)
                    ring_wait(st)
                    o = ring_bank(st)
                    for t in range(4):
                        for kt in range(KT):
                            r = product(o[:, t * NE:(t + 1) * NE], [v[:, kt, b, t * P:(t + 1) * P] for v in xt_hl],
                                        [rw[:, u, kt, :] for u in range(2)], kt == 0, kt == KT - 1)
                    r.then_inc(ring_full, 1)
                elif st[0] == "h":
                    p = st[1]
                    tb, k = pairs[p]
                    if p == 0:
                        pe.wait_ge(exp_done, 2 * NU)
                        pe.wait_ge(w_split, NSW)
                    if p == 1:
                        pe.wait_ge(u_ready, NG)
                    if tb and k == 0:
                        pe.wait_ge(ring_empty, ring_at[("xpose2", 1)] + 1)
                    if p >= 2:
                        if pairs[p - 2][1] < 4:
                            pe.wait_ge(h_free[p % 2], shared_before(pairs, p - 2))
                        else:
                            pe.wait_ge(g_ready, entry_of_pair(p - 2) + 2)
                    q = tb * NE + k - 4
                    if k >= 4:
                        pe.wait_ge(w_split, NSW + 2 * q + 2)
                    for i in range(2):
                        for kt in range(KT):
                            if k < 4:
                                w, c0 = SWH[:, 2 * i + kt, :], k * P
                            else:
                                w, c0 = R1[:, (2 * q) % EW, :], kt * D + i * P
                            r = product(bank[2 * (p % 2) + i], [w[:, u * N + c0:u * N + c0 + P] for u in range(2)],
                                        [v[:, kt, tb, :] for v in xt_hl], kt == 0, kt == KT - 1)
                    r.then_inc(h_full, 1)
                elif st[0] == "y":
                    y = st[1]
                    tb, k = y // (NE + 1), y % (NE + 1)
                    ring_wait(st)
                    ents = [tb * (4 + 2 * NE) + i for i in (range(4) if k == 0 else (2 + 2 * k, 3 + 2 * k))]
                    pe.wait_ge(ht_ready, ents[-1] + 1)
                    for t in range(4):
                        o = ring_bank(st, t // 2)[:, (t % 2) * D:(t % 2 + 1) * D]
                        for i, e in enumerate(ents):
                            if k == 0:
                                w, c0 = SWH[:, 4 + i // 2, :], (i % 2) * D
                            else:
                                w, c0 = R1[:, (2 * (tb * NE + k - 1) + 1) % EW, :], i * D
                            r = product(o, [h[:, t * P:(t + 1) * P] for h in hid[e % HR]],
                                        [w[:, u * N + c0:u * N + c0 + D] for u in range(2)],
                                        i == 0, i == len(ents) - 1)
                    r.then_inc(ring_full, 1)


def raw(ap):
    return ap.bitcast(F32)


def shared_before(pairs, p):
    return sum(1 for i in range(p + 1) if i % 2 == p % 2 and pairs[i][1] < 4)


_OUTS = [((1024, 256), 'float32')]


def kernel(**inputs):
    import numpy as _np
    import concourse.bacc as _bacc
    from concourse import mybir as _mybir
    from concourse.bass_utils import run_bass_kernel_spmd as _run

    nc = _bacc.Bacc("TRN2", target_bir_lowering=False, num_devices=1)
    a = {k: _np.asarray(v) for k, v in inputs.items()}

    def by_d(v):
        return v.reshape(-1, HG, GH, DK).transpose(0, 1, 3, 2).reshape(v.shape)

    def padded(v):
        rows = v.reshape(HG, GH, DK, -1).transpose(1, 2, 0, 3)
        out = _np.zeros((GH, 32, HG, v.shape[-1]), v.dtype)
        out[:, :DK] = rows
        return out.reshape(P, HG, -1)

    data = {
        "x": a["x"].reshape(B * S, D),
        "ctxT": a["ctx_1024"].reshape(B * T, D).T,
        "wqT": by_d(a["L0_xattn_W_Q"].T), "wkT": by_d(a["L0_xattn_W_K"].T), "wvT": a["L0_xattn_W_V"].T,
        "woP": padded(a["L0_xattn_W_O"].T),
        "smalls": _np.concatenate([
            by_d(a["L0_xattn_b_Q"]).reshape(KT, P).T, by_d(a["L0_xattn_b_K"]).reshape(KT, P).T,
            padded(a["L0_xattn_b_V"][:, None])[:, :, 0],
            a["L0_ffn_router_w"].T.reshape(KT, P, NE).transpose(1, 0, 2).reshape(P, KT * NE)], axis=1),
        "bias_rows": _np.concatenate([a["L0_xattn_b_O"], a["L0_ffn_router_bias"]]),
        "sw1": a["L0_ffn_sw1"], "sw3": a["L0_ffn_sw3"], "sw2": a["L0_ffn_sw2"],
        "ew1": a["L0_ffn_ew1"], "ew2": a["L0_ffn_ew2"],
    }
    arrays, args = {}, []
    for name, v in data.items():
        v = _np.ascontiguousarray(v)
        arrays[f"in_{name}_dram"] = v
        args.append(nc.dram_tensor(f"in_{name}_dram", v.shape, _mybir.dt.from_np(v.dtype), kind="ExternalInput").ap())
    args.append(nc.dram_tensor("out_0_dram", (B * S, D), F32, kind="ExternalOutput").ap())
    xattn_ffn(nc, *args)
    r = _run(nc, [arrays], core_ids=[0])
    return r.results[0]["out_0_dram"].reshape(B, S, D)
```

```python
from contextlib import ExitStack

import concourse.bass as bass
from concourse import mybir

F32 = mybir.dt.float32
F32R = mybir.dt.float32r
BF16 = mybir.dt.bfloat16
ALU = mybir.AluOpType
ACT = mybir.ActivationFunctionType
AX = mybir.AxisListType

P = 128
B, S, T, D = 2, 512, 1024, 256
NH, DK = 16, 16
NE, HS = 8, 512
HT = HS // P
N = 512
KT = D // P
GH = 4
NG = B * NH // GH
HG = NH // GH
QT = S // P
KP = T // P // 2
UG = GH * KP
NU = NG * UG
H_FIRST = 8
LEAD = 22
TERMS = 6
KROWS = TERMS * DK
DVE_ENDS = 6
POOL_MID = 6
WARM = 16
EPS = 1e-5
BF16_ONES = 1.0 + 2.0 ** -9 - 2.0 ** -16
SLOTS = 3
PR = 8
HR = 7
EW = 6


def xattn_ffn(nc, x, ctxT, wqT, wkT, wvT, woP, smalls, bias_rows, sw1, sw3, sw2, ew1, ew2, out):
    splits = [("w", 0), ("c", 0, 0), ("c", 0, 1), ("w", 1), ("w", 2), ("c", 1, 0), ("c", 1, 1)]
    jobs = [("T", 0, 0, 0), ("T", 0, 1, 0), ("K", 0, 0, 0), ("K", 0, 0, 1), ("Q", 0, 0, 0),
            ("K", 0, 1, 0), ("K", 0, 1, 1), ("Q", 0, 1, 0)] + [("V", 0, i, 0) for i in range(4)]
    jobs += [("T", 1, 0, 0), ("T", 1, 1, 0)]
    for m in range(2):
        jobs += [("K", 1, m, 0), ("K", 1, m, 1), ("Q", 1, m, 0)]
    jobs += [("B", 0, 0, 0)] + [("V", 1, i, 0) for i in range(4)]
    NJ = len(jobs)
    LAST_KQ = jobs.index(("Q", 1, 1, 0))
    kq_jobs = [j for j in jobs if j[0] in "KQ"]
    kq_of = {j: c for c, j in enumerate(kq_jobs)}

    def job_frees(i, upto):
        return sum(1 for n in range(upto) if n % 4 == i)

    def around_unit(n):
        todo = []
        m = n + LEAD
        if m < NU:
            todo += [("max", m)]
        if n % 2 == 1 and n >= 5:
            q = n // 4 - 1
            if q < NU // 4:
                todo += [("pv", q, (n % 4) // 2)]
        if n % UG == 11 and n // UG + 1 < NG:
            todo += [("negmax", n // UG + 1)]
        g, r = n // UG - 1, n % UG
        if 0 <= g < NG:
            if r == 3:
                todo += [("evac", g)]
            if r == 5:
                todo += [("recip", g)]
            if g < NG - 1:
                if r == 9:
                    todo += [("sums", g)]
                if r == 10:
                    todo += [("norm", g)]
                if r == 14 and g % HG == HG - 1:
                    todo += [("oproj_part", g // HG), ("oproj", g // HG)]
        i = n - (NG - 1) * UG - H_FIRST
        if 0 <= i < 8:
            todo += [("h_part", i // 4, i % 4 // KT, i % KT)]
        r = n - (NG - 2) * UG
        if 1 <= r <= 4:
            todo += [("stats2", 0, r - 1)]
        if r == 5:
            todo += [("var2", 0)]
        if r == 6:
            todo += [("rstd2", 0)]
        if r == 10:
            todo += [("norm2", 0)]
        if r == 14:
            todo += [("xpose2", 0)]
        if 17 <= r <= 20:
            todo += [("logits", 0, r - 17)]
        if r == 22:
            todo += [("router", 0)]
        return todo

    steps = [("stats", 0), ("split", 0), ("rstd", 0), ("split", 1), ("norm1", 0), ("split", 2), ("split", 3)]
    steps += [("job", 0), ("job", 1), ("job", 2), ("mid", 0), ("mid", 1), ("job", 3), ("mid", 2), ("job", 4)]
    steps += [("mid", 3), ("split", 4), ("mid", 4), ("stats", 1), ("job", 5), ("rstd", 1), ("job", 6), ("mid", 5)]
    steps += [("norm1", 1), ("ones", 0), ("job", 7), ("split", 5), ("mid", 6), ("split", 6), ("mid", 7), ("ones", 1)]
    m = 0
    for n in range(8, NJ):
        steps.append(("job", n))
        if n == 13:
            steps.append(("wo",))
        for _ in range(min(2 if n >= 11 else 0, UG - m)):
            steps.append(("max", m))
            m += 1
        if n > 8 and n != LAST_KQ + 1:
            steps.append(("mid", n - 1))
        if n == LAST_KQ:
            steps += [("mid", n)] + [("max", i) for i in range(m, UG)] + [("negmax", 0)]
            m = UG
        if n > LAST_KQ:
            steps.append(("max", m))
            m += 1
    steps += [("mid", NJ - 1), ("clear",), ("ones", 2)] + [("max", i) for i in range(m, LEAD)]
    for n in range(NU + 6):
        if n < NU:
            steps.append(("unit", n))
        steps += around_unit(n)

    pairs = [(tb, k) for tb in range(2) for k in range(HT + NE)]
    steps += [("h_part", i // 4, i % 4 // KT, i % KT) for i in range(8, 16)]
    steps += [("h", 0), ("h", 1), ("sums", NG - 1), ("norm", NG - 1)]
    steps += [("oproj_part", 1)]
    steps += [("h", 2), ("h", 3), ("oproj", 1)]
    for p in range(4, len(pairs)):
        tb, k = pairs[p]
        if p == 6:
            steps += [("stats2", 1, t) for t in range(4)]
        if p == 7:
            steps += [("var2", 1), ("rstd2", 1)]
        if p == 9:
            steps += [("norm2", 1)]
        steps.append(("h", p))
        if p == 10:
            steps += [("xpose2", 1)]
        if p in (13, 14, 15):
            steps += [("logits", 1, p - 13)]
        if p == 15:
            steps += [("logits", 1, 3), ("router", 1)]
        if k == HT:
            steps.append(("y", tb * (NE + 1)))
        elif k > HT:
            steps.append(("y", tb * (NE + 1) + k - HT))
        elif k == 0:
            steps.append(("y", tb * (NE + 1) - 1))
    LAST_Y = 2 * (NE + 1) - 1
    steps.append(("y", LAST_Y))

    ring_at = {}
    for st in steps:
        if st[0] in ("max", "negmax", "sums", "oproj_part", "xpose2", "y"):
            ring_at[st] = len(ring_at)
        if st[0] == "logits" and st[2] == 0:
            ring_at[("router", st[1])] = len(ring_at)
        if st[0] == "oproj_part":
            ring_at[("oproj", st[1])] = ring_at.pop(st)
        if st[0] == "h_part" and st[1] < 2 and st[2:] == (1, 1):
            ring_at[("h", st[1])] = len(ring_at)

    def y_of_entry(i):
        tb, k = i // (HT + 2 * NE), i % (HT + 2 * NE)
        return tb * (NE + 1) + (0 if k < HT else 1 + (k - HT) // 2)

    def entry_of_pair(p):
        tb, k = pairs[p]
        return tb * (HT + 2 * NE) + (k if k < HT else HT + 2 * (k - HT))

    NSW = 6
    NCH = NSW + 2 * 2 * NE
    sw_src = [sw1[0:P, :], sw1[P:D, :], sw3[0:P, :], sw3[P:D, :],
              sw2[0:2 * P, :].rearrange("(k p) n -> p k n", p=P), sw2[2 * P:, :].rearrange("(k p) n -> p k n", p=P)]
    EARLY = NSW + EW

    def chunk_src(c):
        if c < NSW:
            return sw_src[c]
        q = (c - NSW) // 2 % NE
        return (ew1, ew2)[(c - NSW) % 2][q].rearrange("(k p) n -> p k n", p=P)

    with ExitStack() as ctx:
        def sb(name, shape, dt):
            return ctx.enter_context(nc.sbuf_tensor(name, shape, dt))

        def sem(name):
            return ctx.enter_context(nc.semaphore(name))

        psum = ctx.enter_context(nc.psum_tensor("psum", [P, 8, N], F32))
        bank = [psum[:, i, :] for i in range(8)]
        acc = bank[3]

        x_sb = sb("x_sb", [P, 8, D], F32)
        R1 = sb("R1", [P, 8, 1024], F32R)
        SWH = sb("SWH", [P, NSW, 1024], F32R)
        WH = sb("WH", [P, 10, N], F32R)
        XT = sb("XT", [P, 8, N], F32R)
        PB = sb("PB", [P, PR, 2 * N], F32)
        VA = sb("VA", [P, B, 8, NH, DK + 1], F32)
        QS = [sb(f"QS{i}", [P, GH, S], BF16) for i in range(SLOTS)]
        KS = [sb(f"KS{i}", [P, GH, T], BF16) for i in range(SLOTS)]
        RAW = sb("RAW", [P, 2, N], F32)
        TMP = sb("TMP", [P, 4, N], F32)
        PARTS = sb("PARTS", [P, 2, 3, N], BF16)
        parts = [PARTS[:, 0], PARTS[:, 1],
                 RAW[:, :, :].bitcast(BF16).rearrange("p a b -> p (a b)")[:, 0:3 * N]
                 .rearrange("p (i n) -> p i n", i=3)]
        small = sb("small", [P, 4 + HG + KT * NE], F32)
        bqk, bv_sb = small[:, 0:4], small[:, 4:4 + HG]
        rw_raw = small[:, 4 + HG:].rearrange("p (k e) -> p k e", k=KT)
        rows = sb("rows", [P, D + NE], F32)
        bo_sb, rb_sb = rows[:, 0:D], rows[:, D:]
        rw = sb("rw", [P, 2, KT, NE], F32R)
        ident = sb("ident", [P, P], F32)
        identb = sb("identb", [P, P], BF16)
        sel = sb("sel", [P, P], F32)
        stats = sb("stats", [P, 8, 6], F32)
        mv = sb("mv", [P, 8, 2], F32)
        ve = sb("ve", [P, 8], F32)
        std = sb("std", [P, 8], F32)
        rstd0 = sb("rstd0", [P, 8], F32)
        nt1 = sb("nt1", [P, 8], F32)
        nt2 = sb("nt2", [P, 8], F32)
        rstd = sb("rstd", [P, 8], F32)
        negm = sb("negm", [P, 2, GH, QT], F32)
        nhl = sb("nhl", [P, 2, QT, 2, GH], BF16)
        rs = sb("rs", [P, 8, 8], F32)
        desc = sb("desc", [P, NE], F32)
        comb = sb("comb", [P, 8, NE], F32)

        sums16 = sb("sums16", [P, GH * N // P], F32)
        rsum16 = sb("rsum16", [P, GH * N // P], F32)
        xn = KS[2][:, :, :].bitcast(F32).rearrange("p a b -> p (a b)").rearrange("p (t d) -> p t d", d=D)
        craw = PB[:, 0:4, :].rearrange("p a b -> p (a b)").rearrange("p (k t) -> p k t", k=KT)
        wraw = PB[:, 4:6, :].rearrange("p a b -> p (a b)").rearrange("p (w k n) -> p w k n", w=4, k=KT)
        woraw = PB[:, 6, :].rearrange("p (g n) -> p g n", g=HG)
        R1f = R1[:, :, :].rearrange("p a b -> p (a b)")
        ctx_hl = [R1f[:, i * 4096:(i + 1) * 4096].rearrange("p (k t) -> p k t", k=KT) for i in range(2)]
        w_hl = [[WH[:, 2 * w + i, :].rearrange("p (k n) -> p k n", k=KT) for i in range(2)] for w in range(3)]
        WK, WQ, WV = 0, 1, 2
        wo_hl = [WH[:, 6 + 2 * i:8 + 2 * i, :].rearrange("p a b -> p (a b)").rearrange("p (g n) -> p g n", g=HG)
                 for i in range(2)]
        xt_hl = [XT[:, 4 * i:4 * i + 4, :].rearrange("p (k b) n -> p k b n", b=2) for i in range(2)]
        U, RC, RU = TMP[:, 0, :], TMP[:, 1, :], TMP[:, 3, :]
        ao = [[WH[:, 2 * i + u, :] for u in range(2)] for i in range(3)] + [[XT[:, 1, :], XT[:, 3, :]]]
        hid = [[R1[:, 6 + i, u * N:(u + 1) * N] for u in range(2)] for i in range(2)]
        hid += [[WH[:, 2 * i + u, :] for u in range(2)] for i in range(5)]
        nrow = RU[0:2 * GH, :].bitcast(BF16).rearrange("p (b n) -> p b n", b=2)
        rt = QS[2][:, :, :].bitcast(F32).rearrange("p a b -> p (a b)")[:, 0:12 * 8 * NE]\
            .rearrange("p (i t e) -> p i t e", i=12, e=NE)

        qs_d = nc.dram_tensor("qs_d", (B, 2, 3, 2, DK, GH, S), BF16, kind="Internal").ap()
        ks_d = nc.dram_tensor("ks_d", (B, 2, 3, 2, DK, GH, T), BF16, kind="Internal").ap()

        ld_x = [sem(f"ld_x{b}") for b in range(B)]
        ld_ctx = [sem(f"ld_ctx{i}") for i in range(3)]
        ld_w = [sem(f"ld_w{w}") for w in range(3)]
        ld_wo = sem("ld_wo")
        ld_small = sem("ld_small")
        ld_rows = sem("ld_rows")
        consts = sem("consts")
        const_step = sem("const_step")
        ones = sem("ones")
        acc_zero = sem("acc_zero")
        var_ready = sem("var_ready")
        std_ready = sem("std_ready")
        dve_chain = sem("dve_chain")
        xn_ready = sem("xn_ready")
        split_hi = sem("split_hi")
        w_lo = sem("w_lo")
        ctx_lo = sem("ctx_lo")
        pool_split = sem("pool_split")
        pool_chain = sem("pool_chain")
        jobs_done = sem("jobs_done")
        job_free = [sem(f"job_free{i}") for i in range(4)]
        xt_hi = sem("xt_hi")
        kq_hi = sem("kq_hi")
        kq_rest = sem("kq_rest")
        kq_mid = sem("kq_mid")
        kq_split = sem("kq_split")
        kq_stored = [sem(f"kq_stored{c}") for c in range(len(kq_jobs))]
        stk_loaded = [sem(f"stk_loaded{i}") for i in range(SLOTS)]
        bias_loaded = [sem(f"bias_loaded{i}") for i in range(2)]
        ring_full = sem("ring_full")
        ring_empty = sem("ring_empty")
        negm_ready = sem("negm_ready")
        scores_done = sem("scores_done")
        exp_done = sem("exp_done")
        pv_done = sem("pv_done")
        u_ready = sem("u_ready")
        a_hi = sem("a_hi")
        a_lo = sem("a_lo")
        bo_added = sem("bo_added")
        wraw_loaded = [sem(f"wraw_loaded{i}") for i in range(2)]
        w_split = sem("w_split")
        t2_hi = sem("t2_hi")
        rt_logits = sem("rt_logits")
        su_loaded = sem("su_loaded")
        su_recip = sem("su_recip")
        ru_loaded = sem("ru_loaded")
        ru_zero = sem("ru_zero")
        rt_exp = sem("rt_exp")
        h_full = sem("h_full")
        h_free = [sem(f"h_free{i}") for i in range(2)]
        g_ready = sem("g_ready")
        ht_ready = sem("ht_ready")
        stored = sem("stored")
        half_full = sem("half_full")
        half_final = sem("half_final")

        block = ctx.enter_context(nc.Block())

        def ring_bank(st, i=0):
            return bank[4 + 2 * (ring_at[st] % 2) + i]

        def h_bank(p, i):
            return ring_bank(("h", p), i) if p < 2 else bank[2 * (p % 2) + i]

        def kq_count(b, m):
            return 3 * (2 * b + m)

        @block.sync
        def _(sp):
            cT = ctxT.rearrange("(k p) t -> p k t", p=P)
            xt = x.rearrange("(t p) d -> p t d", p=P)
            sp.dma_start(x_sb[:, 0:4, :], xt[:, 0:4, :]).then_inc(ld_x[0], 16)
            sp.dma_start(wraw[:, WK], wkT.rearrange("(k p) n -> p k n", p=P)).then_inc(ld_w[WK], 16)
            for tb in range(2):
                sp.dma_start(craw[:, :, tb * N:(tb + 1) * N], cT[:, :, tb * N:(tb + 1) * N]).then_inc(ld_ctx[tb], 16)
            sp.dma_start(wraw[:, WQ], wqT.rearrange("(k p) n -> p k n", p=P)).then_inc(ld_w[WQ], 16)
            sp.dma_start(small[:, :], smalls).then_inc(ld_small, 16)
            sp.dma_start(x_sb[:, 4:8, :], xt[:, 4:8, :]).then_inc(ld_x[1], 16)
            sp.dma_start(wraw[:, WV], wvT.rearrange("(k p) n -> p k n", p=P)).then_inc(ld_w[WV], 16)
            sp.dma_start(craw[:, :, T:], cT[:, :, T:]).then_inc(ld_ctx[2], 16)
            sp.dma_start(woraw, woP).then_inc(ld_wo, 16)
            sp.dma_start(rows[:, :], bias_rows.rearrange("(a n) -> a n", a=1).broadcast_to([P, D + NE]))\
              .then_inc(ld_rows, 16)

            term_rows = [(3, slice(0, 3 * DK)), (2, slice(3 * DK, 5 * DK)), (1, slice(5 * DK, 6 * DK))]

            def load_stack(g):
                b, hg, s = g // HG, g % HG, g % SLOTS
                stored_k, stored_q = kq_stored[kq_count(b, hg // 2):][:2], kq_stored[kq_count(b, hg // 2) + 2]
                if g == 2:
                    sp.wait_ge(jobs_done, jobs.index(("T", 1, 1, 0)) + 1)
                if g >= SLOTS:
                    sp.wait_ge(scores_done, 2 * UG * (g - SLOTS + 1))
                for loaded in stored_k:
                    sp.wait_ge(loaded, 16)
                for n, rows in term_rows:
                    sp.dma_start(KS[s][rows, :, :].rearrange("r j t -> r (j t)"),
                                 ks_d[b, hg // 2, 0:n, hg % 2].rearrange("p d j t -> p d (j t)"))\
                        .then_inc(stk_loaded[s], 16)
                sp.wait_ge(stored_q, 16)
                for n, rows in term_rows:
                    sp.dma_start(QS[s][rows, :, :].rearrange("r j t -> r (j t)"),
                                 qs_d[b, hg // 2, 3 - n:4 - n, hg % 2].rearrange("o d j t -> o d (j t)")
                                 .broadcast_to([n, DK, GH * S])).then_inc(stk_loaded[s], 16)

            def load_bias(g):
                sp.wait_ge(ring_empty, ring_at[("negmax", g)] + 1)
                for c in range(2):
                    sp.dma_start(QS[g % SLOTS][KROWS + c:KROWS + c + 1, :, :],
                                 nrow[GH * c:GH * c + GH, g % 2, :]).then_inc(bias_loaded[g % 2], 16)

            def load_chunk(c):
                if c == 0:
                    sp.wait_ge(kq_stored[-1], 16)
                if c >= 2:
                    sp.wait_ge(w_split, c - 1)
                dst = RAW[:, c % 2, :]
                if c >= 4:
                    dst = dst.rearrange("p (k n) -> p k n", k=2)
                sp.dma_start(dst, chunk_src(c)).then_inc(wraw_loaded[c % 2], 16)

            for c, (kind, b, m, tb) in enumerate(kq_jobs):
                sp.wait_ge(kq_split, c + 1)
                dst = qs_d[b, m] if kind == "Q" else ks_d[b, m, :, :, :, :, tb * N:(tb + 1) * N]
                sp.dma_start(dst.rearrange("p l d j t -> (l d j) p t"), parts[c % 3])\
                    .then_inc(kq_stored[c], 16)
                if c == 2:
                    load_stack(0)
                if c == 4:
                    load_stack(1)
                if c == 8:
                    load_bias(0)
                    load_stack(2)
            for g in range(NG):
                if g + 1 < NG:
                    load_bias(g + 1)
                if g + SLOTS < NG:
                    load_stack(g + SLOTS)
                sp.wait_ge(u_ready, g + 1)
                sp.dma_start(sums16[:, :], U[DK::32, :]).then_inc(su_loaded, 16)
                sp.wait_ge(su_recip, g + 1)
                sp.dma_start(RU[DK::32, :], rsum16[:, :]).then_inc(ru_loaded, 16)
                for c in range(2 * g, min(2 * g + 2, EARLY)):
                    load_chunk(c)
            for c in range(EARLY, NCH):
                load_chunk(c)
            ot = out.rearrange("(t p) d -> p t d", p=P)
            sp.wait_ge(ring_empty, ring_at[("y", NE)] + 1)
            sp.dma_start(ot[:, 0:4, :], x_sb[:, 0:4, :]).then_inc(stored, 16)
            sp.wait_ge(half_final, 1)
            sp.dma_start(ot[:, 4:6, :], x_sb[:, 4:6, :]).then_inc(stored, 16)
            sp.wait_ge(ring_empty, ring_at[("y", LAST_Y)] + 1)
            sp.dma_start(ot[:, 6:8, :], x_sb[:, 6:8, :]).then_inc(stored, 16)
            sp.wait_ge(stored, 48)

        @block.gpsimd
        def _(pool):
            k = 0
            for t in (ident, identb, sel):
                pool.memset(t[:, :], 0.0).then_inc(const_step, 1)
            pool.wait_ge(const_step, 3)
            for t in (ident, identb):
                pool.affine_select(out=t[:, :], in_=t[:, :], compare_op=ALU.not_equal, fill=1.0, base=0,
                                   pattern=[[-1, P]], channel_multiplier=1).then_inc(consts, 1)
            sv = sel[:, :].rearrange("p (a i) -> p a i", a=4)
            pool.affine_select(out=sv, in_=sv, compare_op=ALU.not_equal, fill=1.0, base=-DK,
                               pattern=[[-32, 4], [0, 32]], channel_multiplier=1).then_inc(consts, 1)
            pool.memset(RU, 0.0).then_inc(ru_zero, 1)
            pool.memset(VA[:, :, :, :, DK:DK + 1], 1.0).then_inc(consts, 1)
            for e in range(NE):
                pool.memset(desc[:, e:e + 1], float(NE - e)).then_inc(consts, 1)

            thirds = 0
            for st in steps:
                if st[0] == "split" and splits[st[1]][0] == "c":
                    _, b, tb = splits[st[1]]
                    c0 = b * T + tb * N
                    pool.wait_ge(split_hi, st[1] + 1)
                    pool.tensor_tensor(ctx_hl[1][:, :, c0:c0 + N], craw[:, :, c0:c0 + N],
                                       raw(ctx_hl[0][:, :, c0:c0 + N]), ALU.subtract).then_inc(ctx_lo, 1)
                    lows = 2 * b + tb + 1
                elif st[0] == "mid" and jobs[st[1]][0] in "KQ":
                    n = st[1]
                    c = kq_of[jobs[n]]
                    if c >= POOL_MID:
                        pool.wait_ge(kq_hi, c + 1)
                        pool.wait_ge(job_free[n % 4], n // 4 + 1)
                        pool.tensor_tensor(TMP[:, c % 3, :], TMP[:, c % 3, :], parts[c % 3][:, 0, :], ALU.subtract)\
                            .then_inc(kq_rest, 1)
                        pool.wait_ge(kq_rest, c - POOL_MID + 1)
                        pool.tensor_scalar(parts[c % 3][:, 1, :], TMP[:, c % 3, :], 1.0, 1.0, ALU.mult, ALU.mult)\
                            .then_inc(kq_mid, 1)
                    pool.wait_ge(kq_mid, c + 1)
                    pool.tensor_tensor(parts[c % 3][:, 2, :], TMP[:, c % 3, :], parts[c % 3][:, 1, :], ALU.subtract)\
                        .then_inc(kq_split, 1)
                    thirds += 1
                elif st[0] == "ones":
                    pool.wait_ge(consts, 3 + 1 + NE)
                    pool.wait_ge(kq_split, thirds)
                    pool.wait_ge(ctx_lo, lows)
                    if st[1] == 2:
                        pool.wait_ge(pool_split, 2)
                        pool.wait_ge(jobs_done, jobs.index(("T", 1, 1, 0)) + 1)
                    pool.memset(KS[st[1]][KROWS:KROWS + 2, :, :].bitcast(F32), BF16_ONES).then_inc(ones, 1)
                    pool.wait_ge(ones, st[1] + 1)
                elif st[0] == "wo":
                    pool.wait_ge(ld_small, 16)
                    pool.tensor_scalar(rw[:, 0], rw_raw, 1.0, 1.0, ALU.mult, ALU.mult).then_inc(pool_chain, 1)
                    pool.wait_ge(ld_wo, 16)
                    pool.tensor_scalar(wo_hl[0], woraw, 1.0, 1.0, ALU.mult, ALU.mult).then_inc(pool_chain, 1)
                    pool.wait_ge(pool_chain, 2)
                    pool.tensor_tensor(rw[:, 1], rw_raw, raw(rw[:, 0]), ALU.subtract).then_inc(pool_split, 1)
                    pool.tensor_tensor(wo_hl[1], woraw, raw(wo_hl[0]), ALU.subtract).then_inc(pool_split, 1)
            pool.wait_ge(xn_ready, 8)
            b_job = jobs.index(("B", 0, 0, 0))
            pool.wait_ge(job_free[b_job % 4], b_job // 4 + 1)
            for t in range(8):
                pool.tensor_tensor(x_sb[:, t, :], x_sb[:, t, :], bo_sb[:, :], ALU.add).then_inc(bo_added, 1)

            def split_chunk(c):
                pool.wait_ge(wraw_loaded[c % 2], 16 * (c // 2 + 1))
                if c < NSW:
                    hi, lo = SWH[:, c, 0:N], SWH[:, c, N:]
                else:
                    s = (c - NSW) % EW
                    hi, lo = R1[:, s, 0:N], R1[:, s, N:]
                    if c == NSW:
                        pool.wait_ge(jobs_done, NJ)
                    if c >= EARLY:
                        q = (c - EARLY) // 2
                        pool.wait_ge(ring_full, ring_at[("y", q // NE * (NE + 1) + 1 + q % NE)] + 1)
                pool.tensor_scalar(hi, RAW[:, c % 2, :], 1.0, 1.0, ALU.mult, ALU.mult).then_inc(pool_chain, 1)
                pool.wait_ge(pool_chain, 3 + c)
                pool.tensor_tensor(lo, RAW[:, c % 2, :], raw(hi), ALU.subtract).then_inc(w_split, 1)

            for g in range(NG):
                for c in range(2 * g, min(2 * g + 2, EARLY)):
                    split_chunk(c)
                pool.wait_ge(a_hi, g + 1)
                pool.tensor_tensor(ao[g % HG][1], RC, raw(ao[g % HG][0]), ALU.subtract).then_inc(a_lo, 1)
            for c in range(EARLY, NCH):
                split_chunk(c)

        @block.scalar
        def _(act):
            def deviation(n, ts):
                act.wait_ge(var_ready, n)
                act.activation(std[:, ts], ve[:, ts], ACT.Sqrt).then_inc(std_ready, 1)

            def split_high(i):
                it = splits[i]
                if it[0] == "w":
                    act.wait_ge(ld_w[it[1]], 16)
                    act.activation(w_hl[it[1]][0], wraw[:, it[1]], ACT.Copy).then_inc(split_hi, 1)
                else:
                    act.wait_ge(ld_ctx[it[2] if it[1] == 0 else 2], 16)
                    c0 = it[1] * T + it[2] * N
                    act.activation(ctx_hl[0][:, :, c0:c0 + N], craw[:, :, c0:c0 + N], ACT.Copy).then_inc(split_hi, 1)

            def job(n):
                kind, b, m, tb = jobs[n]
                if kind == "T":
                    act.wait_ge(jobs_done, n + 1)
                    act.activation(xt_hl[0][:, m, b, :], bank[n % 4][:, :], ACT.Copy).then_inc(xt_hi, 1)
                if kind == "V":
                    act.wait_ge(jobs_done, n + 1)
                    act.activation(VA[:, b, 2 * m:2 * m + 2, :, 0:DK],
                                   bank[n % 4].rearrange("p (t h d) -> p t h d", t=2, h=NH), ACT.Copy)\
                       .then_inc(job_free[n % 4], 1)
                if kind in "KQ":
                    c = kq_of[jobs[n]]
                    act.wait_ge(jobs_done, n + 1)
                    if c == 0:
                        act.wait_ge(ld_small, 16)
                    if c >= 3:
                        act.wait_ge(kq_split, c - 2)
                        act.wait_ge(kq_stored[c - 3], 16)
                    bias = bqk[:, m:m + 1] if kind == "Q" else bqk[:, 2 + m:3 + m]
                    act.activation(TMP[:, c % 3, :], bank[n % 4][:, :], ACT.Identity, bias=bias).then_inc(kq_hi, 1)
                    act.activation(parts[c % 3][:, 0, :], bank[n % 4][:, :], ACT.Identity, bias=bias)\
                        .then_inc(job_free[n % 4], 1)

            def unit(n):
                if n >= PR:
                    act.wait_ge(pv_done, 2 * (n // 4) - 2)
                elif n == 0:
                    act.wait_ge(pool_split, 2)
                    act.wait_ge(w_lo, 3)
                    act.wait_ge(ctx_lo, 4)
                for i in range(2):
                    act.wait_ge(scores_done, 2 * n + i + 1)
                    act.activation(PB[:, n % PR, i * N:(i + 1) * N], bank[(2 * n + i) % 3], ACT.Exp,
                                   scale=DK ** -0.5).then_inc(exp_done, 1)

            def hidden(p):
                tb, k = pairs[p]
                if p < 2:
                    act.wait_ge(ring_full, ring_at[("h", p)] + 1)
                else:
                    act.wait_ge(h_full, p - 1)
                if p == 0:
                    act.wait_ge(pv_done, 2 * (NU // 4 - 1))
                for i in range(1 if k < HT else 2):
                    e = entry_of_pair(p) + i
                    if e >= 4:
                        act.wait_ge(ht_ready, e - 3)
                    act.activation(PB[:, e % 4, N:], h_bank(p, i), ACT.Silu if k < HT else ACT.Gelu)\
                       .then_inc(g_ready, 1)

            for st in steps:
                if st[0] == "split":
                    split_high(st[1])
                elif st[0] == "job":
                    job(st[1])
                elif st[0] in ("rstd", "rstd2"):
                    deviation(st[1] + (1 if st[0] == "rstd" else 3), slice(4 * st[1], 4 * st[1] + 4))
                elif st[0] == "unit":
                    unit(st[1])
                elif st[0] == "evac" and st[1] < DVE_ENDS:
                    g = st[1]
                    act.wait_ge(pv_done, 2 * (g + 1) * KP)
                    if g:
                        act.wait_ge(ring_empty, ring_at[("sums", g - 1)] + 1)
                    else:
                        act.wait_ge(kq_split, len(kq_jobs))
                        act.wait_ge(acc_zero, 1)
                    act.activation(U, acc, ACT.Copy).then_inc(u_ready, 1)
                elif st[0] == "norm" and st[1] < DVE_ENDS:
                    g = st[1]
                    act.wait_ge(ring_empty, ring_at[("sums", g)] + 1)
                    if g == 0:
                        act.wait_ge(jobs_done, NJ)
                    if g == HG:
                        act.wait_ge(ring_full, ring_at[("oproj", 0)] + 1)
                    act.activation(ao[g % HG][0], RC, ACT.Copy).then_inc(a_hi, 1)
                elif st[0] == "xpose2":
                    b = st[1]
                    act.wait_ge(ring_full, ring_at[st] + 1)
                    for i in range(2):
                        act.activation(xt_hl[0][:, i, b, :], ring_bank(st, i), ACT.Copy).then_inc(t2_hi, 1)
                elif st[0] == "router":
                    b = st[1]
                    act.wait_ge(rt_logits, b + 1)
                    act.activation(rt[:, 1, 4 * b:4 * b + 4], rt[:, 0, 4 * b:4 * b + 4], ACT.Exp, scale=-1.0)\
                       .then_inc(rt_exp, 1)
                elif st[0] == "h":
                    hidden(st[1])

        @block.vector
        def _(dve):
            chain = [0]

            def link(ins):
                chain[0] += 1
                ins.then_inc(dve_chain, 1)
                dve.wait_ge(dve_chain, chain[0])


            def variances(b):
                ts = slice(4 * b, 4 * b + 4)
                for t in range(4 * b, 4 * b + 4):
                    last = dve.bn_aggr(mv[:, t, :], stats[:, t, :])
                link(last)
                dve.tensor_scalar(ve[:, ts], mv[:, ts, 1], EPS, None, ALU.add).then_inc(var_ready, 1)

            def refine_rstd(n, ts):
                dve.wait_ge(std_ready, n)
                link(dve.reciprocal(rstd0[:, ts], std[:, ts]))
                link(dve.tensor_tensor(nt1[:, ts], rstd0[:, ts], rstd0[:, ts], ALU.mult))
                link(dve.tensor_tensor(nt2[:, ts], nt1[:, ts], ve[:, ts], ALU.mult))
                link(dve.tensor_scalar(nt1[:, ts], nt2[:, ts], -0.5, 1.5, ALU.mult, ALU.add))
                link(dve.tensor_tensor(rstd[:, ts], rstd0[:, ts], nt1[:, ts], ALU.mult))

            def normalise(t):
                dve.tensor_scalar(xn[:, t, :], x_sb[:, t, :], mv[:, t, 0:1], rstd[:, t:t + 1],
                                  ALU.subtract, ALU.mult).then_inc(xn_ready, 1)

            def split_low(i):
                it = splits[i]
                if it[0] == "w":
                    dve.wait_ge(split_hi, i + 1)
                    dve.tensor_tensor(w_hl[it[1]][1], wraw[:, it[1]], raw(w_hl[it[1]][0]), ALU.subtract)\
                        .then_inc(w_lo, 1)

            def job(n):
                kind, b, m, tb = jobs[n]
                if kind == "T":
                    i = 2 * b + m
                    dve.wait_ge(xt_hi, i + 1)
                    dve.tensor_tensor(xt_hl[1][:, m, b, :], bank[n % 4][:, :], raw(xt_hl[0][:, m, b, :]),
                                      ALU.subtract).then_inc(job_free[n % 4], 1)
                if kind in "KQ" and kq_of[jobs[n]] < POOL_MID:
                    c = kq_of[jobs[n]]
                    dve.wait_ge(kq_hi, c + 1)
                    dve.wait_ge(job_free[n % 4], n // 4 + 1)
                    link(dve.tensor_tensor(TMP[:, c % 3, :], TMP[:, c % 3, :], parts[c % 3][:, 0, :], ALU.subtract))
                    dve.tensor_copy(parts[c % 3][:, 1, :], TMP[:, c % 3, :]).then_inc(kq_mid, 1)
                if kind == "B":
                    dve.wait_ge(jobs_done, n + 1)
                    dve.wait_ge(ld_rows, 16)
                    dve.tensor_tensor(bo_sb[:, :], bank[n % 4][:, 0:D], bo_sb[:, :], ALU.add)\
                       .then_inc(job_free[n % 4], 1)

            def route(st):
                b = st[1]
                ts = slice(4 * b, 4 * b + 4)
                (lg, e_, s_, sel_, eq, w_, oh, oh2, both, prod) = (rt[:, i, ts] for i in range(10))
                dst = comb[:, ts, :]
                if b == 0:
                    dve.wait_ge(consts, 12)
                    dve.wait_ge(ld_rows, 16)
                ring_wait(st)
                src = ring_bank(st)
                dve.tensor_copy(lg, src[:, 0:4 * NE].rearrange("p (t e) -> p t e", e=NE)).then_inc(rt_logits, 1)
                dve.wait_ge(rt_logits, b + 1)
                dve.tensor_copy(rs[:, 0, 0:1], lg[:, 0, 0:1]).then_inc(ring_empty, 1)
                dve.wait_ge(rt_exp, b + 1)
                bc = lambda v: v.broadcast_to([P, 4, NE])
                col = lambda i: rs[:, i, ts].rearrange("p (t o) -> p t o", o=1)
                rbv = rb_sb[:, :].rearrange("p (o e) -> p o e", o=1)
                dsv = desc[:, :].rearrange("p (o e) -> p o e", o=1)
                link(dve.tensor_scalar(both, e_, 1.0, None, ALU.add))
                link(dve.reciprocal(s_, both))
                link(dve.tensor_tensor(sel_, s_, bc(rbv), ALU.add))

                def first_max(oh):
                    link(dve.tensor_reduce(col(0), sel_, AX.X, ALU.max))
                    link(dve.tensor_tensor(eq, sel_, bc(col(0)), ALU.is_equal))
                    link(dve.tensor_tensor(w_, eq, bc(dsv), ALU.mult))
                    link(dve.tensor_reduce(col(1), w_, AX.X, ALU.max))
                    link(dve.tensor_tensor(oh, w_, bc(col(1)), ALU.is_equal))

                first_max(oh)
                link(dve.scalar_tensor_tensor(out=sel_, in0=oh, scalar=-1e30, in1=sel_, op0=ALU.mult, op1=ALU.add))
                first_max(oh2)
                link(dve.tensor_tensor(both, oh, oh2, ALU.add))
                link(dve.tensor_tensor(prod, both, s_, ALU.mult))
                link(dve.tensor_reduce(col(4), prod, AX.X, ALU.add))
                link(dve.tensor_scalar(col(5), col(4), 1e-9, None, ALU.is_gt))
                link(dve.tensor_scalar(col(6), col(4), 1e-9, None, ALU.add))
                link(dve.reciprocal(col(7), col(6)))
                link(dve.tensor_tensor(col(6), col(7), col(5), ALU.mult))
                link(dve.tensor_scalar(col(7), col(5), -0.5, 0.5, ALU.mult, ALU.add))
                link(dve.tensor_tensor(prod, prod, bc(col(6)), ALU.mult))
                link(dve.tensor_tensor(both, both, bc(col(7)), ALU.mult))
                link(dve.tensor_tensor(dst, prod, both, ALU.add))

            def hidden(p):
                tb, k = pairs[p]
                for i in range(1 if k < HT else 2):
                    e = entry_of_pair(p) + i
                    gt = PB[:, e % 4, N:]
                    hi, lo = hid[e % HR]
                    dve.wait_ge(g_ready, e + 1)
                    if k < HT:
                        freed = ring_empty if p < 2 else h_free[p % 2]
                        dve.tensor_tensor(gt, gt, h_bank(p, 1), ALU.mult).then_inc(freed, 1)
                        dve.wait_ge(freed, ring_at[("h", p)] + 1 if p < 2 else shared_before(pairs, p))
                    if e >= HR:
                        dve.wait_ge(ring_full, ring_at[("y", y_of_entry(e - HR))] + 1)
                    elif e == 2:
                        dve.wait_ge(ring_full, ring_at[("oproj", 1)] + 1)
                    link(dve.tensor_copy(hi, gt))
                    dve.tensor_tensor(lo, gt, raw(hi), ALU.subtract).then_inc(ht_ready, 1)

            def add_y(y):
                tb, k = y // (NE + 1), y % (NE + 1)
                if y == LAST_Y:
                    dve.wait_ge(half_full, 1)
                else:
                    ring_wait(("y", y))
                for t in range(4):
                    if y == LAST_Y and t == 2:
                        last.then_inc(half_final, 1)
                        ring_wait(("y", y))
                    src = ring_bank(("y", y), t // 2)[:, (t % 2) * D:(t % 2 + 1) * D]
                    dst = x_sb[:, 4 * tb + t, :]
                    if k == 0:
                        last = dve.tensor_tensor(dst, src, dst, ALU.add)
                    else:
                        last = dve.scalar_tensor_tensor(out=dst, in0=src, scalar=comb[:, 4 * tb + t, k - 1:k],
                                                        in1=dst, op0=ALU.mult, op1=ALU.add)
                last.then_inc(ring_empty, 1)
                dve.wait_ge(ring_empty, ring_at[("y", y)] + 1)

            def ring_wait(st):
                dve.wait_ge(ring_full, ring_at[st] + 1)

            def maxima(m):
                g, r = m // UG, m % UG
                ring_wait(("max", m))
                k0 = 4 + 2 * (ring_at[("max", m)] % 2)
                dve.tensor_reduce(negm[:, g % 2, r // QT, r % QT:r % QT + 1],
                                  psum[:, k0:k0 + 2, :].rearrange("p a n -> p (a n)"), AX.X, ALU.max, negate=True)\
                   .then_inc(ring_empty, 1)
                if r == UG - 1:
                    dve.wait_ge(ring_empty, ring_at[("max", m)] + 1)
                    nv = negm[:, g % 2].rearrange("p j q -> p q j")
                    link(dve.tensor_copy(nhl[:, g % 2, :, 0, :], nv))
                    dve.tensor_tensor(nhl[:, g % 2, :, 1, :], nv, nhl[:, g % 2, :, 0, :], ALU.subtract)\
                       .then_inc(negm_ready, 1)

            def xt_low(i, b, src):
                dve.wait_ge(t2_hi, 2 * b + i + 1)
                return dve.tensor_tensor(xt_hl[1][:, i, b, :], src, raw(xt_hl[0][:, i, b, :]), ALU.subtract)

            for st in steps:
                if st[0] == "mid":
                    job(st[1])
                elif st[0] == "clear":
                    dve.wait_ge(job_free[3], job_frees(3, NJ))
                    dve.memset(acc, 0.0).then_inc(acc_zero, 1)
                elif st[0] == "split":
                    split_low(st[1])
                elif st[0] == "stats":
                    dve.wait_ge(ld_x[st[1]], 16)
                    for t in range(4 * st[1], 4 * st[1] + 4):
                        last = dve.bn_stats(stats[:, t, :], x_sb[:, t, :])
                    link(last)
                    variances(st[1])
                elif st[0] == "norm1":
                    refine_rstd(1 + st[1], slice(4 * st[1], 4 * st[1] + 4))
                    for t in range(4 * st[1], 4 * st[1] + 4):
                        normalise(t)
                elif st[0] == "stats2":
                    b, t = st[1:]
                    dve.wait_ge(ring_empty, ring_at[("oproj", b)] + 1)
                    link(dve.bn_stats(stats[:, 4 * b + t, :], x_sb[:, 4 * b + t, :]))
                elif st[0] == "var2":
                    variances(st[1])
                elif st[0] == "norm2":
                    b = st[1]
                    if b == 0:
                        dve.wait_ge(scores_done, 2 * (NG - 2) * UG)
                    refine_rstd(3 + b, slice(4 * b, 4 * b + 4))
                    for t in range(4 * b, 4 * b + 4):
                        normalise(t)
                elif st[0] == "evac" and st[1] >= DVE_ENDS:
                    g = st[1]
                    dve.wait_ge(pv_done, 2 * (g + 1) * KP)
                    dve.wait_ge(ring_empty, ring_at[("sums", g - 1)] + 1)
                    dve.tensor_copy(U, acc).then_inc(u_ready, 1)
                elif st[0] == "norm" and st[1] >= DVE_ENDS:
                    g = st[1]
                    dve.wait_ge(ring_empty, ring_at[("sums", g)] + 1)
                    dve.tensor_copy(ao[g % HG][0], RC).then_inc(a_hi, 1)
                elif st[0] == "xpose2":
                    b = st[1]
                    ring_wait(st)
                    xt_low(0, b, ring_bank(st, 0))
                    xt_low(1, b, ring_bank(st, 1)).then_inc(ring_empty, 1)
                elif st[0] == "router":
                    route(st)
                elif st[0] == "max":
                    maxima(st[1])
                elif st[0] == "negmax":
                    g = st[1]
                    ring_wait(st)
                    src = ring_bank(st)
                    if g == 0:
                        dve.wait_ge(ru_zero, 1)
                    if g >= 2:
                        dve.wait_ge(bias_loaded[g % 2], 32 * (g // 2))
                    dve.tensor_copy(nrow[:, g % 2, :], src[0:2 * GH, :]).then_inc(ring_empty, 1)
                elif st[0] == "sums":
                    g = st[1]
                    ring_wait(st)
                    src = ring_bank(st)
                    if g:
                        dve.wait_ge(a_lo, g)
                    dve.tensor_tensor(RC, src[:, :], U, ALU.mult).then_inc(ring_empty, 1)
                elif st[0] == "recip":
                    dve.wait_ge(su_loaded, 16 * (st[1] + 1))
                    if st[1]:
                        dve.wait_ge(ru_loaded, 16 * st[1])
                    dve.reciprocal(rsum16[:, :], sums16[:, :]).then_inc(su_recip, 1)
                elif st[0] == "oproj":
                    b = st[1]
                    dve.wait_ge(bo_added, 8)
                    ring_wait(st)
                    for i in range(2):
                        t = 4 * b + 2 * i
                        dst = x_sb[:, t:t + 2, :]
                        src = ring_bank(st, i).rearrange("p (t n) -> p t n", t=2)
                        last = dve.tensor_tensor(dst, src, dst, ALU.add)
                    last.then_inc(ring_empty, 1)

                elif st[0] == "h":
                    hidden(st[1])
                elif st[0] == "y":
                    add_y(st[1])

        @block.tensor
        def _(pe):
            def product(dst, a_hl, b_hl, first=True, last=True):
                for i, (u, v) in enumerate(((0, 0), (0, 1), (1, 0))):
                    r = pe.matmul(dst, a_hl[u], b_hl[v], start=first and i == 0, stop=last and i == 2)
                return r

            def job(n):
                kind, b, m, tb = jobs[n]
                o = bank[n % 4]
                if n >= 4:
                    pe.wait_ge(job_free[n % 4], n // 4)
                if kind == "B":
                    pe.wait_ge(ld_small, 16)
                    pe.wait_ge(ld_wo, 16)
                    for hg in range(HG):
                        r = pe.matmul(o[:, 0:D], bv_sb[:, hg:hg + 1].broadcast_to([P, P]), woraw[:, hg, :],
                                      start=(hg == 0), stop=(hg == HG - 1))
                elif kind == "T":
                    pe.wait_ge(xn_ready, 4 * b + 4)
                    pe.wait_ge(consts, 2)
                    for t in range(4):
                        r = pe.transpose(o[:, t * P:(t + 1) * P], xn[:, 4 * b + t, m * P:(m + 1) * P], ident[:, :])
                elif kind == "K":
                    pe.wait_ge(w_lo, 1)
                    pe.wait_ge(ctx_lo, 2 * b + tb + 1)
                    c0 = b * T + tb * N
                    for kt in range(KT):
                        r = product(o[:, :], [w[:, kt, m * P:(m + 1) * P] for w in w_hl[WK]],
                                    [c[:, kt, c0:c0 + N] for c in ctx_hl], kt == 0, kt == KT - 1)
                elif kind == "Q":
                    pe.wait_ge(w_lo, 2)
                    for kt in range(KT):
                        t = jobs.index(("T", b, kt, 0))
                        pe.wait_ge(job_free[t % 4], t // 4 + 1)
                    for kt in range(KT):
                        r = product(o[:, :], [w[:, kt, m * P:(m + 1) * P] for w in w_hl[WQ]],
                                    [t[:, kt, b, :] for t in xt_hl], kt == 0, kt == KT - 1)
                else:
                    pe.wait_ge(w_lo, 3)
                    pe.wait_ge(ctx_lo, 2 * b + (1 if m < 2 else 2))
                    for t in range(2):
                        c0 = b * T + (2 * m + t) * P
                        for kt in range(KT):
                            r = product(o[:, t * D:(t + 1) * D], [c[:, kt, c0:c0 + P] for c in ctx_hl],
                                        [w[:, kt, :] for w in w_hl[WV]], kt == 0, kt == KT - 1)
                r.then_inc(jobs_done, 1)

            def hidden_part(p, i, kt):
                tb, k = pairs[p]
                if k < HT:
                    w, c0 = SWH[:, 2 * i + kt, :], k * P
                else:
                    w, c0 = R1[:, (2 * (tb * NE + k - HT)) % EW, :], kt * D + i * P
                return product(h_bank(p, i), [w[:, u * N + c0:u * N + c0 + P] for u in range(2)],
                               [v[:, kt, tb, :] for v in xt_hl], kt == 0, kt == KT - 1)

            def ring_wait(st):
                if ring_at[st] >= 2:
                    pe.wait_ge(ring_empty, ring_at[st] - 1)

            pe.wait_ge(consts, 2)
            pe.wait_ge(ru_zero, 1)
            for _ in range(WARM):
                pe.matmul(bank[3], identb[:, :], RU.bitcast(BF16)[:, 0:N], start=True, stop=True)

            for st in steps:
                if st[0] == "job":
                    job(st[1])
                elif st[0] == "unit":
                    n = st[1]
                    g, r = n // UG, n % UG
                    kp, j = r // GH, r % GH
                    s = g % SLOTS
                    if r == 0:
                        pe.wait_ge(bias_loaded[g % 2], 32 * (g // 2 + 1))
                        if g < SLOTS:
                            pe.wait_ge(ones, g + 1)
                        pe.wait_ge(stk_loaded[s], 96 * (g // SLOTS + 1))
                    for i in range(2):
                        t = 2 * n + i
                        if t < 3:
                            pe.wait_ge(job_free[t], job_frees(t, NJ))
                        else:
                            pe.wait_ge(exp_done, t - 2)
                        k0 = (2 * kp + i) * P
                        pe.matmul(bank[t % 3], KS[s][0:KROWS + 2, j, k0:k0 + P], QS[s][0:KROWS + 2, j, :],
                                  start=True, stop=True).then_inc(scores_done, 1)
                elif st[0] == "max":
                    m = st[1]
                    g, r = m // UG, m % UG
                    s, j, qt = g % SLOTS, r // QT, r % QT
                    if r == 0:
                        pe.wait_ge(stk_loaded[s], 96 * (g // SLOTS + 1))
                    ring_wait(st)
                    for half in range(2):
                        last = pe.matmul(ring_bank(st, half), QS[s][0:KROWS, j, qt * P:(qt + 1) * P],
                                         KS[s][0:KROWS, j, half * N:(half + 1) * N], start=True, stop=True)
                    last.then_inc(ring_full, 1)
                elif st[0] == "negmax":
                    g = st[1]
                    ring_wait(st)
                    o = ring_bank(st)
                    pe.wait_ge(negm_ready, g + 1)
                    for qt in range(QT):
                        last = pe.matmul(o[0:2 * GH, qt * P:(qt + 1) * P],
                                         nhl[:, g % 2, qt].rearrange("p c j -> p (c j)"), identb[:, :],
                                         start=True, stop=True)
                    last.then_inc(ring_full, 1)
                elif st[0] == "pv":
                    q, kk = st[1:]
                    g, kp = q // KP, q % KP
                    if kk == 0:
                        pe.wait_ge(exp_done, 2 * (4 * q + 4))
                        if kp == 0:
                            if g:
                                pe.wait_ge(u_ready, g)
                            else:
                                pe.wait_ge(acc_zero, 1)
                    b, hg = g // HG, g % HG
                    for j in range(GH):
                        last = pe.matmul(acc[32 * j:32 * j + DK + 1, :], VA[:, b, 2 * kp + kk, GH * hg + j, :],
                                         PB[:, (4 * q + j) % PR, kk * N:(kk + 1) * N],
                                         start=(kp == 0 and kk == 0), stop=(kp == KP - 1 and kk == 1))
                    last.then_inc(pv_done, 1)
                elif st[0] == "sums":
                    g = st[1]
                    ring_wait(st)
                    o = ring_bank(st)
                    pe.wait_ge(ru_loaded, 16 * (g + 1))
                    pe.matmul(o[:, :], sel[:, :], RU, start=True, stop=True).then_inc(ring_full, 1)
                elif st[0] in ("oproj_part", "oproj"):
                    b = st[1]
                    if st[0] == "oproj_part":
                        groups = range(HG - 1)
                        pe.wait_ge(pool_split, 2)
                        ring_wait(("oproj", b))
                    else:
                        groups = range(HG - 1, HG)
                    pe.wait_ge(a_lo, HG * b + groups[-1] + 1)
                    for i in range(2):
                        o = ring_bank(("oproj", b), i)
                        for t in range(2):
                            t0 = (2 * i + t) * P
                            for hg in groups:
                                last = product(o[:, t * D:(t + 1) * D], [a[:, t0:t0 + P] for a in ao[hg]],
                                               [w[:, hg, :] for w in wo_hl],
                                               t == 0 and hg == 0, t == 1 and hg == HG - 1)
                    if st[0] == "oproj":
                        last.then_inc(ring_full, 1)
                elif st[0] == "xpose2":
                    b = st[1]
                    pe.wait_ge(xn_ready, 8 + 4 * b + 4)
                    ring_wait(st)
                    for i in range(2):
                        for t in range(4):
                            r = pe.transpose(ring_bank(st, i)[:, t * P:(t + 1) * P],
                                             xn[:, 4 * b + t, i * P:(i + 1) * P], ident[:, :])
                    r.then_inc(ring_full, 1)
                elif st[0] == "logits":
                    b, t = st[1:]
                    if t == 0:
                        pe.wait_ge(ring_empty, ring_at[("xpose2", b)] + 1)
                        ring_wait(("router", b))
                    o = ring_bank(("router", b))
                    for kt in range(KT):
                        r = product(o[:, t * NE:(t + 1) * NE], [v[:, kt, b, t * P:(t + 1) * P] for v in xt_hl],
                                    [rw[:, u, kt, :] for u in range(2)], kt == 0, kt == KT - 1)
                    if t == 3:
                        r.then_inc(ring_full, 1)
                elif st[0] == "h":
                    p = st[1]
                    tb, k = pairs[p]
                    if p < 4:
                        continue
                    if tb and k == 0:
                        pe.wait_ge(ring_empty, ring_at[("xpose2", 1)] + 1)
                    if pairs[p - 2][1] < HT:
                        pe.wait_ge(h_free[p % 2], shared_before(pairs, p - 2))
                    else:
                        pe.wait_ge(g_ready, entry_of_pair(p - 2) + 2)
                    q = tb * NE + k - HT
                    if k >= 4:
                        pe.wait_ge(w_split, NSW + 2 * q + 2)
                    for i in range(2):
                        for kt in range(KT):
                            r = hidden_part(p, i, kt)
                    r.then_inc(h_full, 1)
                elif st[0] == "h_part":
                    p, i, kt = st[1:]
                    if (i, kt) == (0, 0):
                        if p < 2:
                            ring_wait(("h", p))
                            pe.wait_ge(w_split, NSW)
                        elif p == 2:
                            pe.wait_ge(exp_done, 2 * NU)
                        else:
                            pe.wait_ge(u_ready, NG)
                    last = hidden_part(p, i, kt)
                    if (i, kt) == (1, 1):
                        last.then_inc(ring_full if p < 2 else h_full, 1)
                elif st[0] == "y":
                    y = st[1]
                    tb, k = y // (NE + 1), y % (NE + 1)
                    ring_wait(st)
                    ents = [tb * (HT + 2 * NE) + i for i in (range(4) if k == 0 else (2 + 2 * k, 3 + 2 * k))]
                    pe.wait_ge(ht_ready, ents[-1] + 1)
                    for t in range(4):
                        o = ring_bank(st, t // 2)[:, (t % 2) * D:(t % 2 + 1) * D]
                        for i, e in enumerate(ents):
                            if k == 0:
                                w, c0 = SWH[:, 4 + i // 2, :], (i % 2) * D
                            else:
                                w, c0 = R1[:, (2 * (tb * NE + k - 1) + 1) % EW, :], i * D
                            r = product(o, [h[:, t * P:(t + 1) * P] for h in hid[e % HR]],
                                        [w[:, u * N + c0:u * N + c0 + D] for u in range(2)],
                                        i == 0, i == len(ents) - 1)
                        if y == LAST_Y and t == 1:
                            r.then_inc(half_full, 1)
                    r.then_inc(ring_full, 1)


def raw(ap):
    return ap.bitcast(F32)


def shared_before(pairs, p):
    return sum(1 for i in range(2, p + 1) if i % 2 == p % 2 and pairs[i][1] < HT)


_OUTS = [((1024, 256), 'float32')]


def kernel(**inputs):
    import numpy as _np
    import concourse.bacc as _bacc
    from concourse import mybir as _mybir
    from concourse.bass_utils import run_bass_kernel_spmd as _run

    nc = _bacc.Bacc("TRN2", target_bir_lowering=False, num_devices=1)
    a = {k: _np.asarray(v) for k, v in inputs.items()}

    def by_d(v):
        return v.reshape(-1, HG, GH, DK).transpose(0, 1, 3, 2).reshape(v.shape)

    def padded(v):
        rows = v.reshape(HG, GH, DK, -1).transpose(1, 2, 0, 3)
        out = _np.zeros((GH, 32, HG, v.shape[-1]), v.dtype)
        out[:, :DK] = rows
        return out.reshape(P, HG, -1)

    data = {
        "x": a["x"].reshape(B * S, D),
        "ctxT": a["ctx_1024"].reshape(B * T, D).T,
        "wqT": by_d(a["L0_xattn_W_Q"].T), "wkT": by_d(a["L0_xattn_W_K"].T), "wvT": a["L0_xattn_W_V"].T,
        "woP": padded(a["L0_xattn_W_O"].T),
        "smalls": _np.concatenate([
            by_d(a["L0_xattn_b_Q"]).reshape(KT, P).T, by_d(a["L0_xattn_b_K"]).reshape(KT, P).T,
            padded(a["L0_xattn_b_V"][:, None])[:, :, 0],
            a["L0_ffn_router_w"].T.reshape(KT, P, NE).transpose(1, 0, 2).reshape(P, KT * NE)], axis=1),
        "bias_rows": _np.concatenate([a["L0_xattn_b_O"], a["L0_ffn_router_bias"]]),
        "sw1": a["L0_ffn_sw1"], "sw3": a["L0_ffn_sw3"], "sw2": a["L0_ffn_sw2"],
        "ew1": a["L0_ffn_ew1"], "ew2": a["L0_ffn_ew2"],
    }
    arrays, args = {}, []
    for name, v in data.items():
        v = _np.ascontiguousarray(v)
        arrays[f"in_{name}_dram"] = v
        args.append(nc.dram_tensor(f"in_{name}_dram", v.shape, _mybir.dt.from_np(v.dtype), kind="ExternalInput").ap())
    args.append(nc.dram_tensor("out_0_dram", (B * S, D), F32, kind="ExternalOutput").ap())
    xattn_ffn(nc, *args)
    r = _run(nc, [arrays], core_ids=[0])
    return r.results[0]["out_0_dram"].reshape(B, S, D)
```
